# Optimizing a Trainium2 kernel written in Bass

```python
import numpy as np
import jax
import jax.numpy as jnp

def _softmax(x, axis=-1):
    return jax.nn.softmax(x, axis=axis)

def _gelu(x):
    return jax.nn.gelu(x, approximate=True)

def _silu(x):
    return jax.nn.silu(x)

def _sigmoid(x):
    return jax.nn.sigmoid(x)

def _layernorm(x, axis=-1, eps=1e-05):
    m = jnp.mean(x, axis=axis, keepdims=True)
    v = jnp.var(x, axis=axis, keepdims=True)
    return (x - m) / jnp.sqrt(v + eps)

def _scatter_add(tgt, idx, src, axis=0):
    return tgt.at[idx].add(src)

def _segment_sum(src, seg, n):
    return jax.ops.segment_sum(src, seg, n)
kernel_name = 'mk_conv_seq_d4_conv_nchw1024_r4_b827c9'

def setup_inputs(seed: int=0):
    np.random.seed(seed)
    _w = jnp.asarray

    def _rec_inputs():
        import jax
        import jax.numpy as jnp
        _gk = jax.random.key(seed)
        x = -0.0003929 + 0.9999 * jax.random.normal(jax.random.fold_in(_gk, 1), (1, 256, 32, 32), jnp.float32)
        return x
    x = _rec_inputs()

    def _L0_conv_setup():
        import jax, jax.numpy as jnp
        import numpy as np
        G = 4

        def _expand_mask(mask, c, H, W):
            b, g, m, _ = mask.shape
            m1 = jnp.repeat(mask, c // g, axis=1)
            m1 = jnp.repeat(jnp.repeat(m1, H // m, axis=2), W // m, axis=3)
            return m1

        def _gconv(x, w, pad):
            return jax.lax.conv_general_dilated(x, w, window_strides=(1, 1), padding=[(pad, pad), (pad, pad)], dimension_numbers=('NCHW', 'OIHW', 'NCHW'), feature_group_count=G)
        key = jax.random.key(seed)
        k1, k2, k3, k4, k5 = jax.random.split(key, 5)
        x = jax.random.normal(k1, (1, 256, 32, 32), dtype=jnp.float32)
        mask = jax.random.bernoulli(k2, 0.5, (1, 4, 8, 8)).astype(jnp.float32)
        w1 = jax.random.normal(k3, (64, 64, 1, 1), dtype=jnp.float32) * 0.05
        w2 = jax.random.normal(k4, (64, 16, 3, 3), dtype=jnp.float32) * 0.05
        w3 = jax.random.normal(k5, (256, 16, 1, 1), dtype=jnp.float32) * 0.05
        return {'x': x, 'mask': mask, 'w1': w1, 'w2': w2, 'w3': w3}
    _L0_conv_all = _L0_conv_setup()
    _L0_conv_in = {k: v for k, v in _L0_conv_all.items() if k in ('mask', 'w1', 'w2', 'w3')}
    del _L0_conv_all

    def _L1_conv_setup():
        import jax, jax.numpy as jnp
        import numpy as np

        def conv(x, w, stride=1, pad=0):
            return jax.lax.conv_general_dilated(x, w, (stride, stride), [(pad, pad), (pad, pad)], dimension_numbers=('NCHW', 'OIHW', 'NCHW'))

        def group_norm(x, scale, bias, groups=32, eps=1e-05):
            B, C, H, W = x.shape
            xg = x.reshape(B, groups, C // groups, H, W)
            m = xg.mean(axis=(2, 3, 4), keepdims=True)
            v = xg.var(axis=(2, 3, 4), keepdims=True)
            xn = ((xg - m) * jax.lax.rsqrt(v + eps)).reshape(B, C, H, W)
            return xn * scale[None, :, None, None] + bias[None, :, None, None]

        def bilinear_sample(x, py, px):
            B, C, H, W = x.shape
            y0 = jnp.floor(py)
            x0 = jnp.floor(px)
            wy1 = py - y0
            wx1 = px - x0
            xf = x.reshape(B, C, H * W)
            Ksp = py.shape[1:]

            def corner(yi, xi, wy, wx):
                valid = (yi >= 0) & (yi < H) & (xi >= 0) & (xi < W)
                yc = jnp.clip(yi, 0, H - 1).astype(jnp.int32)
                xc = jnp.clip(xi, 0, W - 1).astype(jnp.int32)
                idx = (yc * W + xc).reshape(B, 1, -1)
                v = jnp.take_along_axis(xf, idx, axis=2).reshape(B, C, *Ksp)
                w = (wy * wx * valid).astype(x.dtype)[:, None]
                return v * w
            return corner(y0, x0, 1.0 - wy1, 1.0 - wx1) + corner(y0, x0 + 1, 1.0 - wy1, wx1) + corner(y0 + 1, x0, wy1, 1.0 - wx1) + corner(y0 + 1, x0 + 1, wy1, wx1)
        key = jax.random.key(seed)
        ks = jax.random.split(key, 8)
        B, Cin, H, W = (4, 256, 16, 16)
        Cb = 64
        x = jax.random.normal(ks[0], (B, Cin, H, W), dtype=jnp.float32)
        w1 = jax.random.normal(ks[1], (Cb, Cin, 1, 1), dtype=jnp.float32) * (1.0 / np.sqrt(Cin))
        w_off = jax.random.normal(ks[2], (27, Cb, 3, 3), dtype=jnp.float32) * 0.01
        b_off = jnp.zeros((27,), dtype=jnp.float32)
        w2 = jax.random.normal(ks[3], (Cb, Cb, 3, 3), dtype=jnp.float32) * (1.0 / np.sqrt(Cb * 9))
        w3 = jax.random.normal(ks[4], (Cin, Cb, 1, 1), dtype=jnp.float32) * (1.0 / np.sqrt(Cb))
        return {'x': x, 'w1': w1, 'gn1_scale': jnp.ones((Cb,), jnp.float32), 'gn1_bias': jnp.zeros((Cb,), jnp.float32), 'w_off': w_off, 'b_off': b_off, 'w2': w2, 'gn2_scale': jnp.ones((Cb,), jnp.float32), 'gn2_bias': jnp.zeros((Cb,), jnp.float32), 'w3': w3, 'gn3_scale': jnp.ones((Cin,), jnp.float32), 'gn3_bias': jnp.zeros((Cin,), jnp.float32), 'stride': 4}
    _L1_conv_all = _L1_conv_setup()
    _L1_conv_in = {k: v for k, v in _L1_conv_all.items() if k in ('w1', 'gn1_scale', 'gn1_bias', 'w_off', 'b_off', 'w2', 'gn2_scale', 'gn2_bias', 'w3', 'gn3_scale', 'gn3_bias')}
    del _L1_conv_all

    def _L2_conv_setup():
        import jax, jax.numpy as jnp
        import numpy as np
        from jax import lax
        N, CIN, H, W = (4, 256, 56, 56)
        CB = 64
        K = 9

        def _conv(x, w, b, stride=1, padding='SAME'):
            y = lax.conv_general_dilated(x, w, (stride, stride), padding, dimension_numbers=('NCHW', 'OIHW', 'NCHW'))
            return y + b[None, :, None, None]

        def _bilinear_gather(feat, ys, xs):
            n, c, h, w = feat.shape
            y0 = jnp.floor(ys)
            x0 = jnp.floor(xs)
            wy1 = ys - y0
            wy0 = 1.0 - wy1
            wx1 = xs - x0
            wx0 = 1.0 - wx1
            flat = feat.reshape(n, c, h * w)

            def g(yi, xi):
                valid = (yi >= 0) & (yi <= h - 1) & (xi >= 0) & (xi <= w - 1)
                yc = jnp.clip(yi, 0, h - 1).astype(jnp.int32)
                xc = jnp.clip(xi, 0, w - 1).astype(jnp.int32)
                idx = yc * w + xc
                vals = jnp.take_along_axis(flat, idx[:, None, :], axis=2)
                return vals * valid[:, None, :].astype(feat.dtype)
            out = g(y0, x0) * (wy0 * wx0)[:, None, :] + g(y0, x0 + 1) * (wy0 * wx1)[:, None, :] + g(y0 + 1, x0) * (wy1 * wx0)[:, None, :] + g(y0 + 1, x0 + 1) * (wy1 * wx1)[:, None, :]
            return out

        def _deform_conv3x3(feat, w, b, w_off, b_off):
            n, c, h, ww = feat.shape
            off = _conv(feat, w_off, b_off)
            off = off.reshape(n, K, 2, h, ww)
            dy, dx = (off[:, :, 0], off[:, :, 1])
            ki, kj = jnp.meshgrid(jnp.arange(3), jnp.arange(3), indexing='ij')
            ky = (ki.reshape(-1) - 1).astype(feat.dtype)
            kx = (kj.reshape(-1) - 1).astype(feat.dtype)
            hh = jnp.arange(h, dtype=feat.dtype)
            wc = jnp.arange(ww, dtype=feat.dtype)
            ys = hh[None, None, :, None] + ky[None, :, None, None] + dy
            xs = wc[None, None, None, :] + kx[None, :, None, None] + dx
            sampled = _bilinear_gather(feat, ys.reshape(n, -1), xs.reshape(n, -1))
            sampled = sampled.reshape(n, c, K, h, ww)
            out = jnp.einsum('nckhw,ock->nohw', sampled, w.reshape(w.shape[0], c, K))
            return out + b[None, :, None, None]
        key = jax.random.key(seed)
        ks = jax.random.split(key, 6)
        x = jax.random.normal(ks[0], (N, CIN, H, W), dtype=jnp.float32)
        w1 = jax.random.normal(ks[1], (CB, CIN, 1, 1), dtype=jnp.float32) * 0.02
        b1 = jnp.zeros((CB,), jnp.float32)
        w_off = jax.random.normal(ks[2], (2 * K, CB, 3, 3), dtype=jnp.float32) * 0.01
        b_off = jnp.zeros((2 * K,), jnp.float32)
        w2 = jax.random.normal(ks[3], (CB, CB, 3, 3), dtype=jnp.float32) * 0.02
        b2 = jnp.zeros((CB,), jnp.float32)
        w3 = jax.random.normal(ks[4], (CIN, CB, 1, 1), dtype=jnp.float32) * 0.02
        b3 = jnp.zeros((CIN,), jnp.float32)
        return {'x': x, 'w1': w1, 'b1': b1, 'w_off': w_off, 'b_off': b_off, 'w2': w2, 'b2': b2, 'w3': w3, 'b3': b3}
    _L2_conv_all = _L2_conv_setup()
    _L2_conv_in = {k: v for k, v in _L2_conv_all.items() if k in ('w1', 'b1', 'w_off', 'b_off', 'w2', 'b2', 'w3', 'b3')}
    del _L2_conv_all

    def _L3_conv_setup():
        import jax, jax.numpy as jnp
        import numpy as np
        BN_EPS = 1e-05

        def conv1x1(x, w, b):
            return jnp.einsum('bchw,oc->bohw', x, w) + b[None, :, None, None]
        key = jax.random.key(seed)
        ks = jax.random.split(key, 11)
        B, C, H, W = (8, 256, 16, 32)
        hid = 16
        s = 0.02
        return {'x': jax.random.normal(ks[0], (B, C, H, W), dtype=jnp.float32), 'theta_w': jax.random.normal(ks[1], (hid, C), dtype=jnp.float32) * s, 'theta_b': jax.random.normal(ks[2], (hid,), dtype=jnp.float32) * s, 'phi_w': jax.random.normal(ks[3], (hid, C), dtype=jnp.float32) * s, 'phi_b': jax.random.normal(ks[4], (hid,), dtype=jnp.float32) * s, 'g_w': jax.random.normal(ks[5], (hid, C), dtype=jnp.float32) * s, 'g_b': jax.random.normal(ks[6], (hid,), dtype=jnp.float32) * s, 'w_w': jax.random.normal(ks[7], (C, hid), dtype=jnp.float32) * s, 'w_b': jax.random.normal(ks[8], (C,), dtype=jnp.float32) * s, 'bn_gamma': jax.random.normal(ks[9], (C,), dtype=jnp.float32) * 0.1 + 1.0, 'bn_beta': jax.random.normal(ks[10], (C,), dtype=jnp.float32) * 0.1}
    _L3_conv_all = _L3_conv_setup()
    _L3_conv_in = {k: v for k, v in _L3_conv_all.items() if k in ('theta_w', 'theta_b', 'phi_w', 'phi_b', 'g_w', 'g_b', 'w_w', 'w_b', 'bn_gamma', 'bn_beta')}
    del _L3_conv_all
    return {'x': x, 'L0_conv_mask': _L0_conv_in['mask'], 'L0_conv_w1': _L0_conv_in['w1'], 'L0_conv_w2': _L0_conv_in['w2'], 'L0_conv_w3': _L0_conv_in['w3'], 'L1_conv_w1': _L1_conv_in['w1'], 'L1_conv_gn1_scale': _L1_conv_in['gn1_scale'], 'L1_conv_gn1_bias': _L1_conv_in['gn1_bias'], 'L1_conv_w_off': _L1_conv_in['w_off'], 'L1_conv_b_off': _L1_conv_in['b_off'], 'L1_conv_w2': _L1_conv_in['w2'], 'L1_conv_gn2_scale': _L1_conv_in['gn2_scale'], 'L1_conv_gn2_bias': _L1_conv_in['gn2_bias'], 'L1_conv_w3': _L1_conv_in['w3'], 'L1_conv_gn3_scale': _L1_conv_in['gn3_scale'], 'L1_conv_gn3_bias': _L1_conv_in['gn3_bias'], 'L2_conv_w1': _L2_conv_in['w1'], 'L2_conv_b1': _L2_conv_in['b1'], 'L2_conv_w_off': _L2_conv_in['w_off'], 'L2_conv_b_off': _L2_conv_in['b_off'], 'L2_conv_w2': _L2_conv_in['w2'], 'L2_conv_b2': _L2_conv_in['b2'], 'L2_conv_w3': _L2_conv_in['w3'], 'L2_conv_b3': _L2_conv_in['b3'], 'L3_conv_theta_w': _L3_conv_in['theta_w'], 'L3_conv_theta_b': _L3_conv_in['theta_b'], 'L3_conv_phi_w': _L3_conv_in['phi_w'], 'L3_conv_phi_b': _L3_conv_in['phi_b'], 'L3_conv_g_w': _L3_conv_in['g_w'], 'L3_conv_g_b': _L3_conv_in['g_b'], 'L3_conv_w_w': _L3_conv_in['w_w'], 'L3_conv_w_b': _L3_conv_in['w_b'], 'L3_conv_bn_gamma': _L3_conv_in['bn_gamma'], 'L3_conv_bn_beta': _L3_conv_in['bn_beta']}

def reference(x, L0_conv_mask, L0_conv_w1, L0_conv_w2, L0_conv_w3, L1_conv_w1, L1_conv_gn1_scale, L1_conv_gn1_bias, L1_conv_w_off, L1_conv_b_off, L1_conv_w2, L1_conv_gn2_scale, L1_conv_gn2_bias, L1_conv_w3, L1_conv_gn3_scale, L1_conv_gn3_bias, L2_conv_w1, L2_conv_b1, L2_conv_w_off, L2_conv_b_off, L2_conv_w2, L2_conv_b2, L2_conv_w3, L2_conv_b3, L3_conv_theta_w, L3_conv_theta_b, L3_conv_phi_w, L3_conv_phi_b, L3_conv_g_w, L3_conv_g_b, L3_conv_w_w, L3_conv_w_b, L3_conv_bn_gamma, L3_conv_bn_beta):
    import jax
    import jax.numpy as jnp

    def _L0_conv_ref(x, mask, w1, w2, w3):
        import jax, jax.numpy as jnp
        import numpy as np
        G = 4

        def _expand_mask(mask, c, H, W):
            b, g, m, _ = mask.shape
            m1 = jnp.repeat(mask, c // g, axis=1)
            m1 = jnp.repeat(jnp.repeat(m1, H // m, axis=2), W // m, axis=3)
            return m1

        def _gconv(x, w, pad):
            return jax.lax.conv_general_dilated(x, w, window_strides=(1, 1), padding=[(pad, pad), (pad, pad)], dimension_numbers=('NCHW', 'OIHW', 'NCHW'), feature_group_count=G)
        b, c, H, W = x.shape
        residual = x
        m1 = _expand_mask(mask, c, H, W)
        out = x * m1
        out = jax.nn.relu(_gconv(out, w1, 0))
        m2 = _expand_mask(mask, out.shape[1], H, W)
        out = out * m2
        out = jax.nn.relu(_gconv(out, w2, 1))
        out = out * m2
        out = _gconv(out, w3, 0)
        out = out + residual
        return jax.nn.relu(out)

    def _L1_conv_ref(x, w1, gn1_scale, gn1_bias, w_off, b_off, w2, gn2_scale, gn2_bias, w3, gn3_scale, gn3_bias, stride):
        import jax, jax.numpy as jnp
        import numpy as np

        def conv(x, w, stride=1, pad=0):
            return jax.lax.conv_general_dilated(x, w, (stride, stride), [(pad, pad), (pad, pad)], dimension_numbers=('NCHW', 'OIHW', 'NCHW'))

        def group_norm(x, scale, bias, groups=32, eps=1e-05):
            B, C, H, W = x.shape
            xg = x.reshape(B, groups, C // groups, H, W)
            m = xg.mean(axis=(2, 3, 4), keepdims=True)
            v = xg.var(axis=(2, 3, 4), keepdims=True)
            xn = ((xg - m) * jax.lax.rsqrt(v + eps)).reshape(B, C, H, W)
            return xn * scale[None, :, None, None] + bias[None, :, None, None]

        def bilinear_sample(x, py, px):
            B, C, H, W = x.shape
            y0 = jnp.floor(py)
            x0 = jnp.floor(px)
            wy1 = py - y0
            wx1 = px - x0
            xf = x.reshape(B, C, H * W)
            Ksp = py.shape[1:]

            def corner(yi, xi, wy, wx):
                valid = (yi >= 0) & (yi < H) & (xi >= 0) & (xi < W)
                yc = jnp.clip(yi, 0, H - 1).astype(jnp.int32)
                xc = jnp.clip(xi, 0, W - 1).astype(jnp.int32)
                idx = (yc * W + xc).reshape(B, 1, -1)
                v = jnp.take_along_axis(xf, idx, axis=2).reshape(B, C, *Ksp)
                w = (wy * wx * valid).astype(x.dtype)[:, None]
                return v * w
            return corner(y0, x0, 1.0 - wy1, 1.0 - wx1) + corner(y0, x0 + 1, 1.0 - wy1, wx1) + corner(y0 + 1, x0, wy1, 1.0 - wx1) + corner(y0 + 1, x0 + 1, wy1, wx1)
        out = conv(x, w1)
        out = jax.nn.relu(group_norm(out, gn1_scale, gn1_bias))
        om = conv(out, w_off, pad=1) + b_off[None, :, None, None]
        K = 9
        off_x = om[:, :K]
        off_y = om[:, K:2 * K]
        mask = jax.nn.sigmoid(om[:, 2 * K:])
        B, C, H, W = out.shape
        ky, kx = jnp.meshgrid(jnp.arange(3), jnp.arange(3), indexing='ij')
        ky = (ky.reshape(K) - 1).astype(om.dtype)
        kx = (kx.reshape(K) - 1).astype(om.dtype)
        grid_y = jnp.arange(H, dtype=om.dtype)[None, :, None] + ky[:, None, None]
        grid_x = jnp.arange(W, dtype=om.dtype)[None, None, :] + kx[:, None, None]
        py = grid_y[None] + off_y
        px = grid_x[None] + off_x
        sampled = bilinear_sample(out, py, px) * mask[:, None]
        out = jnp.einsum('bckhw,ock->bohw', sampled, w2.reshape(w2.shape[0], w2.shape[1], K))
        out = jax.nn.relu(group_norm(out, gn2_scale, gn2_bias))
        out = conv(out, w3)
        out = group_norm(out, gn3_scale, gn3_bias)
        return jax.nn.relu(out + x)

    def _L2_conv_ref(x, w1, b1, w_off, b_off, w2, b2, w3, b3):
        import jax, jax.numpy as jnp
        import numpy as np
        from jax import lax
        N, CIN, H, W = (4, 256, 56, 56)
        CB = 64
        K = 9

        def _conv(x, w, b, stride=1, padding='SAME'):
            y = lax.conv_general_dilated(x, w, (stride, stride), padding, dimension_numbers=('NCHW', 'OIHW', 'NCHW'))
            return y + b[None, :, None, None]

        def _bilinear_gather(feat, ys, xs):
            n, c, h, w = feat.shape
            y0 = jnp.floor(ys)
            x0 = jnp.floor(xs)
            wy1 = ys - y0
            wy0 = 1.0 - wy1
            wx1 = xs - x0
            wx0 = 1.0 - wx1
            flat = feat.reshape(n, c, h * w)

            def g(yi, xi):
                valid = (yi >= 0) & (yi <= h - 1) & (xi >= 0) & (xi <= w - 1)
                yc = jnp.clip(yi, 0, h - 1).astype(jnp.int32)
                xc = jnp.clip(xi, 0, w - 1).astype(jnp.int32)
                idx = yc * w + xc
                vals = jnp.take_along_axis(flat, idx[:, None, :], axis=2)
                return vals * valid[:, None, :].astype(feat.dtype)
            out = g(y0, x0) * (wy0 * wx0)[:, None, :] + g(y0, x0 + 1) * (wy0 * wx1)[:, None, :] + g(y0 + 1, x0) * (wy1 * wx0)[:, None, :] + g(y0 + 1, x0 + 1) * (wy1 * wx1)[:, None, :]
            return out

        def _deform_conv3x3(feat, w, b, w_off, b_off):
            n, c, h, ww = feat.shape
            off = _conv(feat, w_off, b_off)
            off = off.reshape(n, K, 2, h, ww)
            dy, dx = (off[:, :, 0], off[:, :, 1])
            ki, kj = jnp.meshgrid(jnp.arange(3), jnp.arange(3), indexing='ij')
            ky = (ki.reshape(-1) - 1).astype(feat.dtype)
            kx = (kj.reshape(-1) - 1).astype(feat.dtype)
            hh = jnp.arange(h, dtype=feat.dtype)
            wc = jnp.arange(ww, dtype=feat.dtype)
            ys = hh[None, None, :, None] + ky[None, :, None, None] + dy
            xs = wc[None, None, None, :] + kx[None, :, None, None] + dx
            sampled = _bilinear_gather(feat, ys.reshape(n, -1), xs.reshape(n, -1))
            sampled = sampled.reshape(n, c, K, h, ww)
            out = jnp.einsum('nckhw,ock->nohw', sampled, w.reshape(w.shape[0], c, K))
            return out + b[None, :, None, None]
        r = jax.nn.relu(_conv(x, w1, b1))
        r = jax.nn.relu(_deform_conv3x3(r, w2, b2, w_off, b_off))
        r = _conv(r, w3, b3)
        return jax.nn.relu(x + r)

    def _L3_conv_ref(x, theta_w, theta_b, phi_w, phi_b, g_w, g_b, w_w, w_b, bn_gamma, bn_beta):
        import jax, jax.numpy as jnp
        import numpy as np
        BN_EPS = 1e-05

        def conv1x1(x, w, b):
            return jnp.einsum('bchw,oc->bohw', x, w) + b[None, :, None, None]
        B, C, H, W = x.shape
        hid = theta_w.shape[0]
        N = H * W
        theta = conv1x1(x, theta_w, theta_b).reshape(B, hid, N).transpose(0, 2, 1)
        phi = conv1x1(x, phi_w, phi_b).reshape(B, hid, N)
        g = conv1x1(x, g_w, g_b).reshape(B, hid, N).transpose(0, 2, 1)
        f = jnp.einsum('bnd,bdm->bnm', theta, phi) / N
        y = jnp.einsum('bnm,bmd->bnd', f, g)
        y = y.transpose(0, 2, 1).reshape(B, hid, H, W)
        wy = conv1x1(y, w_w, w_b)
        mean = wy.mean(axis=(0, 2, 3), keepdims=True)
        var = wy.var(axis=(0, 2, 3), keepdims=True)
        norm = (wy - mean) * jax.lax.rsqrt(var + BN_EPS)
        out = norm * bn_gamma[None, :, None, None] + bn_beta[None, :, None, None]
        return out + x

    def _gn(v, G=32, eps=1e-05):
        B_, C_, H_, W_ = v.shape
        g = v.reshape(B_, G, C_ // G, H_, W_)
        m = jnp.mean(g, axis=(2, 3, 4), keepdims=True)
        s = jnp.var(g, axis=(2, 3, 4), keepdims=True)
        return ((g - m) / jnp.sqrt(s + eps)).reshape(v.shape)

    def _ln_c(v, eps=1e-06):
        m = jnp.mean(v, axis=1, keepdims=True)
        s = jnp.var(v, axis=1, keepdims=True)
        return (v - m) / jnp.sqrt(s + eps)

    def _ln_t(v, eps=1e-05):
        m = jnp.mean(v, axis=-1, keepdims=True)
        s = jnp.var(v, axis=-1, keepdims=True)
        return (v - m) / jnp.sqrt(s + eps)

    def _to_tokens(v):
        B_, C_, H_, W_ = v.shape
        return v.reshape(B_, C_, H_ * W_).transpose(0, 2, 1)

    def _from_tokens(t, like):
        B_, C_, H_, W_ = like.shape
        return t.transpose(0, 2, 1).reshape(B_, C_, H_, W_)
    x = _L0_conv_ref(x, L0_conv_mask, L0_conv_w1, L0_conv_w2, L0_conv_w3)
    x = _L1_conv_ref(x, L1_conv_w1, L1_conv_gn1_scale, L1_conv_gn1_bias, L1_conv_w_off, L1_conv_b_off, L1_conv_w2, L1_conv_gn2_scale, L1_conv_gn2_bias, L1_conv_w3, L1_conv_gn3_scale, L1_conv_gn3_bias, 4)
    x = _L2_conv_ref(x, L2_conv_w1, L2_conv_b1, L2_conv_w_off, L2_conv_b_off, L2_conv_w2, L2_conv_b2, L2_conv_w3, L2_conv_b3)
    x = _L3_conv_ref(x, L3_conv_theta_w, L3_conv_theta_b, L3_conv_phi_w, L3_conv_phi_b, L3_conv_g_w, L3_conv_g_b, L3_conv_w_w, L3_conv_w_b, L3_conv_bn_gamma, L3_conv_bn_beta)
    return x

_drawn_inputs = setup_inputs


def setup_inputs(seed=0):
    import zlib

    import numpy as np

    out = dict(_drawn_inputs(seed))
    spreads = {'L1_conv_gn1_scale': (1.0, 0.2),
     'L1_conv_gn1_bias': (0.0, 0.1),
     'L1_conv_b_off': (0.0, 0.1),
     'L1_conv_gn2_scale': (1.0, 0.2),
     'L1_conv_gn2_bias': (0.0, 0.1),
     'L1_conv_gn3_scale': (1.0, 0.2),
     'L1_conv_gn3_bias': (0.0, 0.1),
     'L2_conv_b1': (0.0, 0.8),
     'L2_conv_b_off': (0.0, 0.8),
     'L2_conv_b2': (0.0, 0.8),
     'L2_conv_b3': (0.0, 0.1)}
    factors = {'L0_conv_w1': 3.808,
     'L0_conv_w2': 3.423,
     'L0_conv_w3': 3.009,
     'L2_conv_w1': 7.512,
     'L2_conv_w_off': 8.0,
     'L2_conv_w2': 4.704,
     'L2_conv_w3': 3.688,
     'L3_conv_theta_b': 64.0,
     'L3_conv_w_b': 64.0,
     'L3_conv_phi_b': 3.83}
    for name, (base, spread) in spreads.items():
        noise = np.random.default_rng([zlib.crc32(name.encode()), seed]).standard_normal(out[name].shape)
        drawn = base * np.exp(spread * noise) if base else spread * noise
        out[name] = jnp.asarray(drawn.astype(out[name].dtype))
    for name, factor in factors.items():
        out[name] = (out[name] * factor).astype(out[name].dtype)
    return out
```

```python
from contextlib import ExitStack

import concourse.bass as bass
from concourse import mybir

F32 = mybir.dt.float32
I32 = mybir.dt.int32
ALU = mybir.AluOpType
ACT = mybir.ActivationFunctionType

P = 128
C = 256
CT = C // P
H = W = 32
N = H * W
HALF = N // 2
TILES = N // P
ROWS = P // W
HID = 64
TAPS = 9
TAPSETS = 6
PAIRS = TAPS // 2
CORNERS = 4
PATCH = CORNERS * HID
PW = W + 2
GROUPS0 = 4
G0 = HID // GROUPS0
D = 16
EPS = 1e-5
MAGIC = 1.5 * 2.0 ** 23
RUN = N // P
RING = 5
TPAD = H

FIRST = [("w1c", CT * G0), ("w1m", CT * GROUPS0), ("mask", 64), ("w2c", TAPSETS * G0),
         ("w2m", GROUPS0), ("w3c", HID), ("w3m", GROUPS0), ("ident", P)]
SECOND = [("g2", P), ("g8", P), ("base", 3 * TILES * TAPS),
          ("b1w1", CT * P), ("b1off", 6 * 27), ("b1boff", 27), ("b1w2", 5 * HID), ("b1w3", C),
          ("gn1s", 1), ("gn1b", 1), ("gn2s", 1), ("gn2b", 1), ("gn3s", CT), ("gn3b", CT),
          ("b2w1", CT * P), ("b2off", 6 * 18), ("b2boff", 18), ("b2w2", 5 * HID), ("b2w3", C),
          ("b2b1", 1), ("b2b2", 1), ("b2b3", CT),
          ("pgw", CT * 2 * D), ("pgb", 2 * D), ("thw", CT * D), ("thb", 1), ("www", C),
          ("bns", CT), ("bnb", CT)]



B_C1 = 0
B_OM = 2
B_W4 = 3
B_ST = 4
B_ST1 = 6
B_C3 = 4


def width(fields):
    return sum(n for _, n in fields)


def conv_chain(nc, x_in, first_in, second_in, wb_in, out):
    with ExitStack() as ctx:
        def sb(name, shape, dt=F32):
            return ctx.enter_context(nc.sbuf_tensor(name, shape, dt))

        def sem(name):
            return ctx.enter_context(nc.semaphore(name))

        x0 = sb("x0", [P, CT, N])
        x1 = sb("x1", [P, CT, N])
        x2 = sb("x2", [P, CT, N])
        x3 = sb("x3", [P, CT, N])
        yo = sb("yo", [P, CT, N])
        first = sb("first", [P, width(FIRST)])
        second = sb("second", [P, width(SECOND)])
        fld = {}
        for tile, fields in ((first, FIRST), (second, SECOND)):
            at = 0
            for name, n in fields:
                fld[name] = tile[:, at:at + n]
                at += n
        ident = fld["ident"]

        mask_x = sb("mask_x", [P, 8, W])
        mask = sb("mask", [P, N])
        w1bd = sb("w1bd", [P, CT, 2, GROUPS0, G0])
        w2bd = sb("w2bd", [P, TAPSETS, GROUPS0, G0])
        w3bd = sb("w3bd", [HID, GROUPS0, HID])
        pad = sb("pad", [P, PW, PW])
        img = sb("img", [P, PW, W])
        left = sb("left", [HID, PW, W])
        m0 = sb("m0", [P, N])
        hid = [sb(f"hid{b}", [HID, N]) for b in range(3)]
        feat_t = sb("feat_t", [P, RUN + 1, HID])
        bias_pos = [sb(f"bias_pos{b}", [P, 3, TILES, TAPS]) for b in range(2)]
        pos = sb("pos", [P, 3, TILES * TAPS])
        low = sb("low", [P, 2, TILES * TAPS])
        row_y = sb("row_y", [P, TILES * TAPS])
        dist = sb("dist", [P, 2, TILES * TAPS])
        absd = sb("absd", [P, 2, 2, TILES * TAPS])
        hat = sb("hat", [P, 2, 2, TILES * TAPS])
        sig = sb("sig", [P, TILES * TAPS])
        hat_m = sb("hat_m", [P, 2, TILES * TAPS])
        idx = [sb(f"idx{b}", [P, TILES * TAPS], I32) for b in range(2)]
        G = sb("G", [P, RING, TAPS, PATCH])
        GW = sb("GW", [P, 2, CORNERS, TAPS, HID])
        sT = sb("sT", [P, PAIRS + 1, N])
        st = sb("st", [P, CT, 2, 6])
        mv = sb("mv", [P, CT, 2])
        gm = sb("gm", [P, CT, 2])
        var = sb("var", [P, CT])
        rstd = sb("rstd", [P, CT])
        sc = sb("sc", [P, CT])
        nb = sb("nb", [P, CT])
        zeros = sb("zeros", [TPAD, P])
        half_neg = sb("half_neg", [P, CT])
        pg = sb("pg", [P, TILES, 2 * D])
        th = sb("th", [2 * D, N])
        mt = sb("mt", [D, D])
        at_w = sb("at_w", [D + 1, C])
        ps = ctx.enter_context(nc.psum_tensor("ps", [P, 8, 512], F32))
        table = [nc.dram_tensor(f"table{b}", (TPAD + N, PATCH), F32, kind="Internal").ap()
                 for b in range(2)]

        s_first, s_second, s_wb = sem("s_first"), sem("s_second"), sem("s_wb")
        s_x = [sem(f"s_x{t}") for t in range(CT)]
        s_zero = sem("s_zero")
        s_const = sem("s_const")
        s_mask = sem("s_mask")
        s_wbd = sem("s_wbd")
        s_d = sem("s_d")
        s_c1 = [sem(f"s_c1_{b}") for b in range(3)]
        s_pad = [sem(f"s_pad{b}") for b in range(3)]
        s_right = [sem(f"s_right{b}") for b in range(3)]
        s_left = [sem(f"s_left{b}") for b in range(3)]
        s_c2 = [sem(f"s_c2_{b}") for b in range(3)]
        s_hid = [sem(f"s_hid{b}") for b in range(3)]
        s_c3 = [sem(f"s_c3_{b}") for b in range(3)]
        s_t = [sem(f"s_t{b}") for b in range(3)]
        s_xa = [sem(f"s_xa{b}") for b in range(3)]
        s_xd = [sem(f"s_xd{b}") for b in range(3)]
        s_mv = sem("s_mv")
        s_gm = sem("s_gm")
        s_var = sem("s_var")
        s_pow = sem("s_pow")
        s_sb = sem("s_sb")
        s_tr = sem("s_tr")
        s_om = sem("s_om")
        s_ftA, s_ftD = sem("s_ftA"), sem("s_ftD")
        s_tab = [sem(f"s_tab{b}") for b in range(2)]
        s_pos, s_idx, s_dist, s_abs = sem("s_pos"), sem("s_idx"), sem("s_dist"), sem("s_abs")
        s_hat, s_sig, s_w4 = sem("s_hat"), sem("s_sig"), sem("s_w4")
        s_gather = [[sem(f"s_gather{b}_{t}") for t in range(TILES)] for b in range(2)]
        s_gw = sem("s_gw")
        s_st = sem("s_st")
        s_sT = sem("s_sT")
        s_pgm, s_pg = sem("s_pgm"), sem("s_pg")
        s_thm, s_th = sem("s_thm"), sem("s_th")
        s_mtm, s_mt, s_atm, s_at = sem("s_mtm"), sem("s_mt"), sem("s_atm"), sem("s_at")
        s_wy, s_fin, s_yo, s_out = sem("s_wy"), sem("s_fin"), sem("s_yo"), sem("s_out")
        block = ctx.enter_context(nc.Block())

        def half(ap, h):
            return ap[:, h * HALF:(h + 1) * HALF]

        def interior(h, upper):
            p0, r0 = (HID, 0) if upper else (0, 1)
            r0 += h * H // 2
            return pad[p0:p0 + HID, r0:r0 + H // 2, 1:1 + W]

        def half_rows(h):
            return slice(1 + h * H // 2, 1 + (h + 1) * H // 2)

        def as_rows(ap):
            return ap.rearrange("p (y x) -> p y x", x=W)

        def quarter(m, h):
            return ps[:, B_C3 + 2 * m + h, :]

        QUARTERS = [(h, m) for h in range(2) for m in range(CT)]

        def table_view(tab, row, side):
            return tab[row:row + N, side * P:(side + 1) * P].rearrange("(p j) e -> p j e", j=RUN)

        def table_source():
            ap = feat_t[:, 0:RUN, :]
            return bass.AP(ap.tensor, ap.offset, [list(ap.ap[0]), [HID, RUN], [1, 2 * HID]])

        @block.sync
        def _(sp):
            sp.dma_start(first[:], first_in).then_inc(s_first, 16)
            sp.dma_start(x0[:, 1, :], x_in[1]).then_inc(s_x[1], 16)
            sp.dma_start(second[:], second_in).then_inc(s_second, 16)
            sp.dma_start(at_w[D:D + 1, :], wb_in).then_inc(s_wb, 16)
            sp.wait_ge(s_zero, 1)
            for b in range(2):
                sp.dma_start(table[b][0:TPAD, 0:P], zeros[:]).then_inc(s_tab[b], 16)
                sp.dma_start(table[b][N:N + TPAD, P:PATCH], zeros[:]).then_inc(s_tab[b], 16)
            for b in range(2):
                sp.wait_ge(s_ftA, b + 1)
                sp.wait_ge(s_ftD, b + 1)
                sp.dma_start(table_view(table[b], TPAD, 0), table_source()).then_inc(s_tab[b], 16)
            for q, (h, m) in enumerate(QUARTERS):
                if q % 2 == 0:
                    sp.wait_ge(s_yo, q + 1)
                    sp.dma_start(half(out[m], h), half(yo[:, m, :], h)).then_inc(s_out, 16)
            sp.wait_ge(s_out, 16 * len(QUARTERS))

        @block.gpsimd
        def _(pool):
            pool.memset(zeros[:], 0.0).then_inc(s_zero, 1)
            for border in (pad, img, left):
                pool.memset(border[:], 0.0).then_inc(s_const, 1)
            pool.memset(half_neg[:], -0.5).then_inc(s_const, 1)
            pool.memset(th[:], 1.0).then_inc(s_const, 1)
            pool.wait_ge(s_first, 16)
            m8 = fld["mask"].rearrange("p (y x) -> p y x", x=8)
            pool.tensor_copy(mask_x[:].rearrange("p y (x r) -> p (y x) r", r=4),
                             fld["mask"][:, :, None].to_broadcast([P, 64, 4])).then_inc(s_mask, 1)
            pool.wait_ge(s_mask, 1)
            pool.tensor_copy(mask[:].rearrange("p (y r x) -> p y r x", r=4, x=W),
                             mask_x[:, :, None, :].to_broadcast([P, 8, 4, W])).then_inc(s_mask, 1)

            def power(norm, p, m):
                pool.wait_ge(s_var, norm)
                pool.tensor_tensor(rstd[0:p, 0:m], var[0:p, 0:m], half_neg[0:p, 0:m],
                                   ALU.pow).then_inc(s_pow, 1)

            def gathers(b):
                pool.wait_ge(s_idx, b + 1)
                pool.wait_ge(s_tab[b], 64)
                for t in range(TILES):
                    done = b * TILES + t
                    if done >= RING:
                        pool.wait_ge(s_gw, done - RING + 1)
                    for k in range(TAPS):
                        n = t * TAPS + k
                        pool.indirect_dma_start(
                            out=G[:, done % RING, k, :], out_offset=None, in_=table[b],
                            in_offset=bass.IndirectOffsetOnAxis(ap=idx[b][:, n:n + 1], axis=0),
                        ).then_inc(s_gather[b][t], 16)

            def left_copy(b):
                for h in range(2):
                    pool.wait_ge(s_pad[b], h + 1)
                    pool.tensor_copy(left[:, half_rows(h), 0:W - 1],
                                     img[HID:P, half_rows(h), 1:W]).then_inc(s_left[b], 1)

            power(1, P, 1)
            left_copy(1)
            gathers(0)
            power(2, HID, 1)
            power(3, P, CT)
            left_copy(2)
            gathers(1)
            power(4, P, CT)

        @block.vector
        def _(dve):
            steps = [0]

            def then(ins):
                steps[0] += 1
                ins.then_inc(s_d, 1)
                dve.wait_ge(s_d, steps[0])

            def channel_stats(norm, p, m):
                for i in range(m):
                    then(dve.bn_aggr(mv[0:p, i, :], st[0:p, i, :, :].rearrange("p a b -> p (a b)")))
                for i in range(m):
                    ins = dve.scalar_tensor_tensor(out=mv[0:p, i, 1:2], in0=mv[0:p, i, 0:1],
                                                   scalar=mv[0:p, i, 0:1], in1=mv[0:p, i, 1:2],
                                                   op0=ALU.mult, op1=ALU.add)
                    ins.then_inc(s_mv, 1) if i == m - 1 else then(ins)

            def scale_bias(norm, p, m, stats, gamma, beta):
                dve.wait_ge(s_pow, norm)
                then(dve.tensor_tensor(sc[0:p, 0:m], rstd[0:p, 0:m], gamma, ALU.mult))
                then(dve.tensor_tensor(nb[0:p, 0:m], stats, sc[0:p, 0:m], ALU.mult))
                dve.tensor_tensor(nb[0:p, 0:m], beta, nb[0:p, 0:m], ALU.subtract).then_inc(s_sb, 1)
                dve.wait_ge(s_sb, norm)

            def group_norm(norm, p, m, gamma, beta):
                dve.wait_ge(s_gm, norm)
                then(dve.tensor_copy(gm[0:p, 0:m, :],
                                     ps[0:p, B_OM, 0:2 * m].rearrange("p (m s) -> p m s", s=2)))
                then(dve.tensor_tensor(var[0:p, 0:m], gm[0:p, 0:m, 0], gm[0:p, 0:m, 0], ALU.mult))
                then(dve.tensor_tensor(var[0:p, 0:m], gm[0:p, 0:m, 1], var[0:p, 0:m], ALU.subtract))
                dve.tensor_scalar(var[0:p, 0:m], var[0:p, 0:m], EPS, None, ALU.add).then_inc(s_var, 1)
                scale_bias(norm, p, m, gm[0:p, 0:m, 0], gamma, beta)

            dve.wait_ge(s_first, 16)
            w1c = fld["w1c"].rearrange("p (t o) -> p t o", t=CT)
            w1m = fld["w1m"].rearrange("p (t g) -> p t g", t=CT)
            for twice in range(2):
                dve.tensor_tensor(w1bd[:, :, twice],
                                  w1c[:, :, None, :].to_broadcast([P, CT, GROUPS0, G0]),
                                  w1m[:, :, :, None].to_broadcast([P, CT, GROUPS0, G0]),
                                  ALU.mult).then_inc(s_wbd, 1)
            w2c = fld["w2c"].rearrange("p (t o) -> p t o", t=TAPSETS)
            dve.tensor_tensor(w2bd[:], w2c[:, :, None, :].to_broadcast([P, TAPSETS, GROUPS0, G0]),
                              fld["w2m"][:, None, :, None].to_broadcast([P, TAPSETS, GROUPS0, G0]),
                              ALU.mult).then_inc(s_wbd, 1)
            dve.tensor_tensor(w3bd[:], fld["w3c"][0:HID, None, :].to_broadcast([HID, GROUPS0, HID]),
                              fld["w3m"][0:HID, :, None].to_broadcast([HID, GROUPS0, HID]),
                              ALU.mult).then_inc(s_wbd, 1)

            dve.wait_ge(s_mask, 2)
            dve.wait_ge(s_const, 5)
            for h in range(2):
                dve.wait_ge(s_c1[0], h + 1)
                then(dve.tensor_tensor(half(m0, h), ps[:, B_C1 + h, :], half(mask, h), ALU.mult))
                for upper in range(2):
                    p0 = HID * upper
                    dve.scalar_tensor_tensor(out=interior(h, upper),
                                             in0=as_rows(half(m0[p0:p0 + HID], h)), scalar=0.0,
                                             in1=as_rows(half(mask[p0:p0 + HID], h)),
                                             op0=ALU.max, op1=ALU.mult).then_inc(s_pad[0], 1)
            dve.wait_ge(s_second, 16)
            base = fld["base"].rearrange("p (a t k) -> p a t k", a=3, k=TAPS)
            for b in range(2):
                bo = fld[f"b{b + 1}boff"].rearrange("p (a k) -> p a k", k=TAPS)
                for a in range(3 - b):
                    then(dve.tensor_tensor(bias_pos[b][:, a], base[:, a],
                                           bo[:, a, None, :].to_broadcast([P, TILES, TAPS]), ALU.add))
            for h in range(2):
                dve.wait_ge(s_c2[0], h + 1)
                dve.scalar_tensor_tensor(out=half(hid[0], h), in0=ps[0:HID, B_OM + h, :], scalar=0.0,
                                         in1=half(mask[0:HID], h), op0=ALU.max,
                                         op1=ALU.mult).then_inc(s_hid[0], 1)
            for q, (h, m) in enumerate(QUARTERS):
                if m:
                    dve.wait_ge(s_c3[0], q + 1)
                    dve.tensor_scalar(half(x1[:, m, :], h), quarter(m, h), 0.0, None,
                                      ALU.max).then_inc(s_xd[0], 1)

            def right_copy(b):
                for h in range(2):
                    dve.wait_ge(s_pad[b], h + 1)
                    dve.tensor_copy(img[0:HID, half_rows(h), 1:W],
                                    img[HID:P, half_rows(h), 0:W - 1]).then_inc(s_right[b], 1)

            def sampling(b):
                axes = 3 - b
                dve.wait_ge(s_tr, b + 1)
                dve.tensor_copy(feat_t[:, RUN, :], ps[:, B_C1 + 1, 0:HID]).then_inc(s_ftD, 1)
                dve.wait_ge(s_om, b + 1)
                if b:
                    dve.wait_ge(s_w4, 1)
                om = ps[:, B_OM, 0:TILES * axes * TAPS].rearrange("p (t a k) -> p t a k", a=axes, k=TAPS)
                for a in range(axes):
                    ins = dve.tensor_tensor(pos[:, a].rearrange("p (t k) -> p t k", k=TAPS),
                                            om[:, :, a, :], bias_pos[b][:, a], ALU.add)
                    ins.then_inc(s_pos, 1)
                dve.wait_ge(s_pos, 3 * b + axes)
                then(dve.tensor_scalar(low[:], pos[:, 0:2], -0.5, 0.0, ALU.add, ALU.max))
                then(dve.tensor_scalar(low[:], low[:], MAGIC, MAGIC + W - 2, ALU.add, ALU.min))
                then(dve.tensor_scalar(row_y[:], low[:, 1], MAGIC - TPAD // W, float(W), ALU.subtract, ALU.mult))
                dve.scalar_tensor_tensor(out=idx[b][:], in0=low[:, 0], scalar=MAGIC, in1=row_y[:],
                                         op0=ALU.subtract, op1=ALU.add).then_inc(s_idx, 1)
                dve.scalar_tensor_tensor(out=dist[:], in0=low[:], scalar=MAGIC, in1=pos[:, 0:2],
                                         op0=ALU.subtract, op1=ALU.subtract).then_inc(s_dist, 1)
                dve.wait_ge(s_hat, b + 1)
                hy = hat[:, :, 1, :]
                if b == 0:
                    dve.wait_ge(s_sig, 1)
                    then(dve.tensor_tensor(hat_m[:], hat[:, :, 1, :],
                                           sig[:, None, :].to_broadcast([P, 2, TILES * TAPS]), ALU.mult))
                    hy = hat_m[:]
                w4 = ps[:, B_W4, 0:TILES * TAPS * CORNERS].rearrange("p (n y x) -> p n y x", x=2, y=2)
                hx = hat[:, :, 0, :]
                dve.tensor_tensor(
                    w4, hx.rearrange("p r n -> p n r")[:, :, None, :].to_broadcast([P, TILES * TAPS, 2, 2]),
                    hy.rearrange("p r n -> p n r")[:, :, :, None].to_broadcast([P, TILES * TAPS, 2, 2]),
                    ALU.mult).then_inc(s_w4, 1)
                dve.wait_ge(s_w4, b + 1)

            def weigh(b):
                for t in range(TILES):
                    done = b * TILES + t
                    dve.wait_ge(s_gather[b][t], 16 * TAPS)
                    if done >= 2:
                        dve.wait_ge(s_st, done - 1)
                    n = TAPS * CORNERS
                    w = ps[:, B_W4, t * n:(t + 1) * n]
                    dve.tensor_tensor(
                        GW[:, t % 2].rearrange("p c k e -> p k c e"),
                        G[:, done % RING].rearrange("p k (c e) -> p k c e", e=HID),
                        w.rearrange("p (k c) -> p k c", c=CORNERS)[:, :, :, None]
                        .to_broadcast([P, TAPS, CORNERS, HID]), ALU.mult).then_inc(s_gw, 1)

            for h in range(2):
                dve.wait_ge(s_c1[1], h + 1)
                then(dve.bn_stats(st[:, 0, h, :], ps[:, B_C1 + h, :]))
            channel_stats(1, P, 1)
            group_norm(1, P, 1, fld["gn1s"], fld["gn1b"])
            right_copy(1)
            sampling(0)
            weigh(0)
            for h in range(2):
                dve.wait_ge(s_c2[1], h + 1)
                then(dve.bn_stats(st[0:HID, 0, h, :], ps[0:HID, B_C1 + h, :]))
            channel_stats(2, HID, 1)
            group_norm(2, HID, 1, fld["gn2s"][0:HID], fld["gn2b"][0:HID])
            for q, (h, m) in enumerate(QUARTERS):
                dve.wait_ge(s_c3[1], q + 1)
                then(dve.bn_stats(st[:, m, h, :], quarter(m, h)))
            channel_stats(3, P, CT)
            group_norm(3, P, CT, fld["gn3s"], fld["gn3b"])
            for h, m in QUARTERS:
                dve.scalar_tensor_tensor(out=half(x2[:, m, :], h), in0=quarter(m, h),
                                         scalar=sc[:, m:m + 1], in1=half(x1[:, m, :], h),
                                         op0=ALU.mult, op1=ALU.add).then_inc(s_t[1], 1)

            right_copy(2)
            sampling(1)
            weigh(1)
            for q, (h, m) in enumerate(QUARTERS):
                if m:
                    dve.wait_ge(s_c3[2], q + 1)
                    dve.tensor_scalar(half(x3[:, m, :], h), quarter(m, h), fld["b2b3"][:, m:m + 1], 0.0,
                                      ALU.add, ALU.max).then_inc(s_xd[2], 1)

            dve.wait_ge(s_pgm, 1)
            dve.tensor_tensor(pg[:], ps[:, B_OM, 0:TILES * 2 * D].rearrange("p (t e) -> p t e", e=2 * D),
                              fld["pgb"][:, None, :].to_broadcast([P, TILES, 2 * D]),
                              ALU.add).then_inc(s_pg, 1)
            dve.wait_ge(s_mtm, 1)
            dve.tensor_scalar(mt[:], ps[0:D, B_W4, 0:D], 1.0 / N, None, ALU.mult).then_inc(s_mt, 1)
            dve.wait_ge(s_atm, 1)
            dve.tensor_copy(at_w[0:D, :], ps[0:D, B_W4, 0:C]).then_inc(s_at, 1)
            for q, (h, m) in enumerate(QUARTERS):
                dve.wait_ge(s_wy, q + 1)
                then(dve.bn_stats(st[:, m, h, :], quarter(m, h)))
            for m in range(CT):
                then(dve.bn_aggr(mv[:, m, :], st[:, m, :, :].rearrange("p a b -> p (a b)")))
            dve.tensor_scalar(var[:], mv[:, :, 1], EPS, None, ALU.add).then_inc(s_var, 1)
            scale_bias(4, P, CT, mv[:, :, 0], fld["bns"], fld["bnb"])
            for q, (h, m) in enumerate(QUARTERS):
                dve.wait_ge(s_fin, q + 1)
                dve.tensor_tensor(half(yo[:, m, :], h), half(yo[:, m, :], h), half(x3[:, m, :], h),
                                  ALU.add).then_inc(s_yo, 1)

        @block.scalar
        def _(act):
            act.dma_start(x0[:, 0, :], x_in[0]).then_inc(s_x[0], 16)
            for q, (h, m) in enumerate(QUARTERS):
                if not m:
                    act.wait_ge(s_c3[0], q + 1)
                    act.activation(half(x1[:, m, :], h), quarter(m, h), ACT.Relu).then_inc(s_xa[0], 1)

            def features(b, scale, bias):
                for h in range(2):
                    act.activation(img[HID:P, half_rows(h), :], as_rows(ps[HID:P, B_C1 + h, :]), ACT.Relu,
                                   scale=scale, bias=bias).then_inc(s_pad[b], 1)

            def sampling(b):
                act.wait_ge(s_tr, b + 1)
                act.activation(feat_t[:, 0:RUN, :], ps[:, B_C1, :].rearrange("p (j e) -> p j e", e=HID),
                               ACT.Copy).then_inc(s_ftA, 1)
                act.wait_ge(s_ftA, b + 1)
                act.wait_ge(s_ftD, b + 1)
                act.dma_start(table_view(table[b], 0, 1), table_source()).then_inc(s_tab[b], 16)
                if b == 0:
                    act.wait_ge(s_pos, 3)
                    act.activation(sig[:], pos[:, 2], ACT.Sigmoid).then_inc(s_sig, 1)
                act.wait_ge(s_dist, b + 1)
                for r in range(2):
                    act.activation(absd[:, r], dist[:], ACT.Abs, bias=float(r)).then_inc(s_abs, 1)
                act.wait_ge(s_abs, 2 * b + 2)
                act.activation(hat[:], absd[:], ACT.Relu, scale=-1.0, bias=1.0).then_inc(s_hat, 1)

            def samples(b):
                for t in range(TILES):
                    done = b * TILES + t
                    act.wait_ge(s_st, done + 1)
                    act.activation(sT[:, 0:PAIRS, t * P:(t + 1) * P],
                                   ps[:, B_ST + t % 2, :].rearrange("p (q n) -> p q n", n=P),
                                   ACT.Copy).then_inc(s_sT, 1)
                    act.activation(sT[0:HID, PAIRS, t * P:(t + 1) * P], ps[0:HID, B_ST1 + t % 2, 0:P],
                                   ACT.Copy).then_inc(s_sT, 1)

            act.wait_ge(s_sb, 1)
            features(1, sc[HID:P, 0:1], nb[HID:P, 0:1])
            sampling(0)
            samples(0)
            act.wait_ge(s_sb, 2)
            for h in range(2):
                act.activation(half(hid[1], h), ps[0:HID, B_C1 + h, :], ACT.Relu,
                               scale=sc[0:HID, 0:1], bias=nb[0:HID, 0:1]).then_inc(s_hid[1], 1)
            for q, (h, m) in enumerate(QUARTERS):
                act.wait_ge(s_t[1], q + 1)
                act.activation(half(x2[:, m, :], h), half(x2[:, m, :], h), ACT.Relu,
                               bias=nb[:, m:m + 1]).then_inc(s_xa[1], 1)

            act.wait_ge(s_c1[2], 2)
            features(2, 1.0, fld["b2b1"][HID:P])
            sampling(1)
            samples(1)
            for h in range(2):
                act.wait_ge(s_c2[2], h + 1)
                act.activation(half(hid[2], h), ps[0:HID, B_C1 + h, :], ACT.Relu,
                               bias=fld["b2b2"][0:HID]).then_inc(s_hid[2], 1)
            for q, (h, m) in enumerate(QUARTERS):
                if not m:
                    act.wait_ge(s_c3[2], q + 1)
                    act.activation(half(x3[:, m, :], h), quarter(m, h), ACT.Relu,
                                   bias=fld["b2b3"][:, m:m + 1]).then_inc(s_xa[2], 1)

            for h in range(2):
                act.wait_ge(s_thm, h + 1)
                act.activation(half(th[0:D], h), ps[0:D, B_C1 + h, :], ACT.Identity,
                               bias=fld["thb"][0:D]).then_inc(s_th, 1)
            act.wait_ge(s_sb, 4)
            for q, (h, m) in enumerate(QUARTERS):
                act.activation(half(yo[:, m, :], h), quarter(m, h), ACT.Identity,
                               scale=sc[:, m:m + 1], bias=nb[:, m:m + 1]).then_inc(s_fin, 1)
                if q % 2:
                    act.wait_ge(s_yo, q + 1)
                    act.dma_start(half(out[m], h), half(yo[:, m, :], h)).then_inc(s_out, 16)

        @block.tensor
        def _(pe):
            def conv1(b, weights, src):
                for h in range(2):
                    for t in range(CT):
                        mm = pe.matmul(ps[:, B_C1 + h, :], weights[:, t, :], half(src[:, t, :], h),
                                       start=(t == 0), stop=(t == CT - 1))
                    mm.then_inc(s_c1[b], 1)

            def tapsets():
                return [(P, 0, kx) for kx in range(3)] + [(HID, 2, kx) for kx in range(3)]

            def residual(src):
                for h, m in QUARTERS:
                    pe.matmul(quarter(m, h), ident, half(src[:, m, :], h), start=True, stop=False)

            def conv3(b, weights, start):
                for h in range(2):
                    pe.wait_ge(s_hid[b], h + 1)
                    for m in range(CT):
                        pe.matmul(quarter(m, h), weights[:, m * P:(m + 1) * P], half(hid[b], h),
                                  start=start, stop=True).then_inc(s_c3[b], 1)

            def group_stats(norm, p, m, matrix):
                pe.wait_ge(s_mv, norm)
                pe.matmul(ps[0:p, B_OM, 0:2 * m], matrix[0:p, 0:p],
                          mv[0:p, 0:m, :].rearrange("p m s -> p (m s)"),
                          start=True, stop=True).then_inc(s_gm, 1)

            def features(b, weights, axes):
                pe.wait_ge(s_pad[b], 2)
                pixels = img[HID:P].rearrange("c y x -> c (y x)")
                for j in range(RUN + 1):
                    tr = pe.transpose(ps[:, B_C1 + j // RUN, (j % RUN) * HID:(j % RUN + 1) * HID],
                                      pixels[:, W + j:W + j + (P - 1) * RUN + 1:RUN], ident[HID:P, HID:P])
                tr.then_inc(s_tr, 1)
                pe.wait_ge(s_right[b], 2)
                pe.wait_ge(s_left[b], 2)
                n = axes * TAPS
                w = weights.rearrange("p (e o) -> p e o", o=n)
                for t in range(TILES):
                    for e in range(TAPSETS):
                        src, p = (img, P) if e < 3 else (left, HID)
                        r = t * ROWS + e % 3
                        om = pe.matmul(ps[:, B_OM, t * n:(t + 1) * n],
                                       src[:, r:r + ROWS, :].rearrange("c y x -> c (y x)"),
                                       w[0:p, e, :], start=(e == 0), stop=(e == TAPSETS - 1))
                om.then_inc(s_om, 1)

            def deform(b, weights):
                w = weights.rearrange("p (q o) -> p q o", o=HID)

                def contract(h):
                    pe.wait_ge(s_sT, 2 * (b * TILES + (h + 1) * TILES // 2))
                    for q in range(PAIRS + 1):
                        p = P if q < PAIRS else HID
                        mm = pe.matmul(ps[0:HID, B_C1 + h, :], w[0:p, q, :], half(sT[0:p, q, :], h),
                                       start=(q == 0), stop=(q == PAIRS))
                    mm.then_inc(s_c2[b + 1], 1)

                for t in range(TILES):
                    done = b * TILES + t
                    pe.wait_ge(s_gw, done + 1)
                    if done >= 2:
                        pe.wait_ge(s_sT, 2 * (done - 1))
                    for q in range(PAIRS + 1):
                        k = 2 * q
                        n = min(2, TAPS - k)
                        dst = ps[:, B_ST + t % 2, q * P:(q + 1) * P] if n == 2 else ps[0:HID, B_ST1 + t % 2, 0:P]
                        for c in range(CORNERS):
                            mm = pe.matmul(dst, GW[:, t % 2, c, k:k + n, :].rearrange("p k e -> p (k e)"), ident,
                                           start=(c == 0), stop=(c == CORNERS - 1))
                    mm.then_inc(s_st, 1)
                    if t == TILES // 2:
                        contract(0)
                contract(1)

            pe.wait_ge(s_wbd, 4)
            for t in range(CT):
                pe.wait_ge(s_x[t], 16)
            conv1(0, w1bd[:].rearrange("p t d g o -> p t (d g o)"), x0)
            residual(x0)
            pe.wait_ge(s_pad[0], 4)
            for h in range(2):
                for e, (p, r, kx) in enumerate(tapsets()):
                    r0 = r + h * H // 2
                    mm = pe.matmul(ps[0:HID, B_OM + h, :], w2bd[0:p, e].rearrange("p g o -> p (g o)"),
                                   pad[0:p, r0:r0 + H // 2, kx:kx + W],
                                   start=(e == 0), stop=(e == TAPSETS - 1))
                mm.then_inc(s_c2[0], 1)
            conv3(0, w3bd[:].rearrange("p g o -> p (g o)"), False)

            pe.wait_ge(s_xa[0], 2)
            pe.wait_ge(s_xd[0], 2)
            pe.wait_ge(s_second, 16)
            conv1(1, fld["b1w1"].rearrange("p (t o) -> p t o", o=P), x1)
            group_stats(1, P, 1, fld["g2"])
            features(1, fld["b1off"], 3)
            deform(0, fld["b1w2"])
            group_stats(2, HID, 1, fld["g2"])
            conv3(1, fld["b1w3"][0:HID], True)
            group_stats(3, P, CT, fld["g8"])

            pe.wait_ge(s_xa[1], 4)
            conv1(2, fld["b2w1"].rearrange("p (t o) -> p t o", o=P), x2)
            features(2, fld["b2off"], 2)
            deform(1, fld["b2w2"])
            residual(x2)
            conv3(2, fld["b2w3"][0:HID], False)

            pgw = fld["pgw"].rearrange("p (t e) -> p t e", e=2 * D)
            thw = fld["thw"].rearrange("p (t e) -> p t e", e=D)
            for h in range(2):
                pe.wait_ge(s_xa[2], h + 1)
                pe.wait_ge(s_xd[2], h + 1)
                for t in range(h * TILES // 2, (h + 1) * TILES // 2):
                    for i in range(CT):
                        mm = pe.matmul(ps[:, B_OM, t * 2 * D:(t + 1) * 2 * D],
                                       x3[:, i, t * P:(t + 1) * P], pgw[:, i, :],
                                       start=(i == 0), stop=(i == CT - 1))
                if h:
                    mm.then_inc(s_pgm, 1)
                for i in range(CT):
                    mm = pe.matmul(ps[0:D, B_C1 + h, :], thw[:, i, :], half(x3[:, i, :], h),
                                   start=(i == 0), stop=(i == CT - 1))
                mm.then_inc(s_thm, 1)
            pe.wait_ge(s_pg, 1)
            for t in range(TILES):
                mm = pe.matmul(ps[0:D, B_W4, 0:D], pg[:, t, D:2 * D], pg[:, t, 0:D],
                               start=(t == 0), stop=(t == TILES - 1))
            mm.then_inc(s_mtm, 1)
            pe.wait_ge(s_mt, 1)
            pe.matmul(ps[0:D, B_W4, 0:C], mt[:], fld["www"][0:D], start=True, stop=True).then_inc(s_atm, 1)
            pe.wait_ge(s_at, 1)
            pe.wait_ge(s_wb, 16)
            pe.wait_ge(s_th, 2)
            for h, m in QUARTERS:
                pe.matmul(quarter(m, h), at_w[:, m * P:(m + 1) * P], half(th[0:D + 1], h),
                          start=True, stop=True).then_inc(s_wy, 1)


def constants():
    import numpy as np

    p = np.arange(P)
    w1m = np.zeros((P, CT, GROUPS0), np.float32)
    for t in range(CT):
        w1m[p, t, 2 * t + p // HID] = 1
    wm = np.zeros((P, GROUPS0), np.float32)
    wm[p, p % HID // G0] = 1
    k = np.arange(TAPS)
    base = np.zeros((P, 3, TILES, TAPS), np.float32)
    t = np.arange(TILES)[None, :, None]
    base[:, 0] = (p % W)[:, None, None] + k % 3 - 1 + 0 * t
    base[:, 1] = (p // W)[:, None, None] + ROWS * t + k // 3 - 1
    return {"w1m": w1m, "w2m": wm, "w3m": wm, "ident": np.eye(P, dtype=np.float32),
            "g2": np.kron(np.eye(P // 2), np.full((2, 2), 1 / 2)).astype(np.float32),
            "g8": np.kron(np.eye(P // 8), np.full((8, 8), 1 / 8)).astype(np.float32),
            "base": base}


def pack(fields, parts):
    import numpy as np

    packed = np.zeros((P, width(fields)), np.float32)
    at = 0
    for name, n in fields:
        a = parts[name]
        a = a.reshape(a.shape[0], -1)
        packed[:a.shape[0], at:at + a.shape[1]] = a
        at += n
    return packed


def lay_out(i):
    import numpy as np

    def col(v):
        return v.reshape(-1, P).T

    def twice(v):
        return np.concatenate([v, v]).reshape(P, 1)

    def tapsets(w):
        top = w[:, :, 0, :].transpose(1, 2, 0)
        mid = w[:, :, 1, :].transpose(1, 2, 0)
        low = w[:, :, 2, :].transpose(1, 2, 0)
        return np.concatenate([np.concatenate([top, low], 1), np.concatenate([mid, np.zeros_like(low)], 1)], 0)

    def tapcols(w):
        return tapsets(w.transpose(0, 1, 3, 2))

    def channels(w):
        return w.reshape(w.shape[0], CT, P).transpose(2, 1, 0)

    def pairs(w):
        w = w.reshape(HID, HID, TAPS).transpose(2, 1, 0)
        w = np.concatenate([w, np.zeros_like(w[:1])], 0)
        return w.reshape(PAIRS + 1, P, HID).transpose(1, 0, 2)

    def rows(v):
        return np.broadcast_to(v.reshape(1, -1), (P, v.size))

    xy = [2 * k + 1 for k in range(TAPS)] + [2 * k for k in range(TAPS)]
    w1 = i["L0_conv_w1"].reshape(CT, 2, G0, HID).transpose(1, 3, 0, 2).reshape(P, CT * G0)
    m = i["L0_conv_mask"].reshape(GROUPS0, 64)
    w3 = i["L0_conv_w3"].reshape(GROUPS0, HID, G0).transpose(0, 2, 1).reshape(HID, HID)
    w2 = tapsets(i["L0_conv_w2"].reshape(GROUPS0, G0, G0, 3, 3).transpose(1, 0, 2, 3, 4)
                 .reshape(G0, HID, 3, 3))
    parts = dict(constants())
    parts.update({
        "w1c": w1, "mask": np.tile(np.repeat(m, G0, 0), (2, 1)), "w2c": w2, "w3c": w3,
        "b1w1": channels(np.tile(i["L1_conv_w1"].reshape(HID, C), (2, 1))), "b1off": tapcols(i["L1_conv_w_off"]),
        "b1boff": rows(i["L1_conv_b_off"]), "b1w2": pairs(i["L1_conv_w2"]),
        "b1w3": i["L1_conv_w3"].reshape(C, HID).T,
        "gn1s": twice(i["L1_conv_gn1_scale"]), "gn1b": twice(i["L1_conv_gn1_bias"]),
        "gn2s": twice(i["L1_conv_gn2_scale"]), "gn2b": twice(i["L1_conv_gn2_bias"]),
        "gn3s": col(i["L1_conv_gn3_scale"]), "gn3b": col(i["L1_conv_gn3_bias"]),
        "b2w1": channels(np.tile(i["L2_conv_w1"].reshape(HID, C), (2, 1))), "b2off": tapcols(i["L2_conv_w_off"][xy]),
        "b2boff": rows(i["L2_conv_b_off"][xy]), "b2w2": pairs(i["L2_conv_w2"]),
        "b2w3": i["L2_conv_w3"].reshape(C, HID).T,
        "b2b1": twice(i["L2_conv_b1"]), "b2b2": twice(i["L2_conv_b2"]), "b2b3": col(i["L2_conv_b3"]),
        "pgw": channels(np.concatenate([i["L3_conv_phi_w"], i["L3_conv_g_w"]])),
        "pgb": rows(np.concatenate([i["L3_conv_phi_b"], i["L3_conv_g_b"]])),
        "thw": channels(i["L3_conv_theta_w"]), "thb": i["L3_conv_theta_b"].reshape(D, 1),
        "www": i["L3_conv_w_w"].T, "bns": col(i["L3_conv_bn_gamma"]), "bnb": col(i["L3_conv_bn_beta"]),
    })
    return {"x": i["x"].reshape(CT, P, N), "first": pack(FIRST, parts), "second": pack(SECOND, parts),
            "w_b": i["L3_conv_w_b"].reshape(1, C)}


def kernel(**inputs):
    import numpy as np
    import concourse.bacc as bacc
    from concourse.bass_utils import run_bass_kernel_spmd as run

    arrays = {f"in_{k}": np.ascontiguousarray(v)
              for k, v in lay_out({k: np.asarray(v) for k, v in inputs.items()}).items()}
    nc = bacc.Bacc("TRN2", target_bir_lowering=False, num_devices=1)
    args = [nc.dram_tensor(k, a.shape, mybir.dt.from_np(a.dtype), kind="ExternalInput").ap()
            for k, a in arrays.items()]
    out = nc.dram_tensor("out", (CT, P, N), F32, kind="ExternalOutput").ap()
    conv_chain(nc, *args, out)
    r = run(nc, [arrays], core_ids=[0])
    return r.results[0]["out"].reshape(1, C, H, W)
```

```python
from contextlib import ExitStack

import concourse.bass as bass
from concourse import mybir

F32 = mybir.dt.float32
F32R = mybir.dt.float32r
I32 = mybir.dt.int32
ALU = mybir.AluOpType
ACT = mybir.ActivationFunctionType

P = 128
C = 256
CT = C // P
H = W = 32
N = H * W
HALF = N // 2
TILES = N // P
ROWS = P // W
HID = 64
TAPS = 9
TAPSETS = 6
PAIRS = TAPS // 2
CORNERS = 4
PATCH = CORNERS * HID
PW = W + 2
GROUPS0 = 4
G0 = HID // GROUPS0
D = 16
EPS = 1e-5
MAGIC = 1.5 * 2.0 ** 23
SLOT = 32
RUN = N // P
RING = 5
TPAD = H

FIRST = [("w1c", CT * G0), ("w1m", CT * GROUPS0), ("mask", 64), ("w2c", TAPSETS * G0),
         ("w2m", GROUPS0), ("w3c", HID), ("w3m", GROUPS0), ("ident", P)]
SECOND = [("g2", P), ("g8", P), ("base", 3 * TILES * TAPS),
          ("b1w1", CT * HID), ("b1off", TAPS * 27), ("b1boff", 27), ("b1w2", 5 * HID), ("b1w3", C),
          ("gn1s", 1), ("gn1b", 1), ("gn2s", 1), ("gn2b", 1), ("gn3s", CT), ("gn3b", CT),
          ("b2w1", CT * HID), ("b2off", TAPS * 18), ("b2boff", 18), ("b2w2", 5 * HID), ("b2w3", C),
          ("b2b1", 1), ("b2b2", 1), ("b2b3", CT),
          ("pgw", CT * 2 * D), ("pgb", 2 * D), ("thw", CT * D), ("thb", 1), ("www", C),
          ("bns", CT), ("bnb", CT)]



B_C1 = 0
B_OM = 2
B_W4 = 3
B_OFF = 4
B_ST = 4
B_ST1 = 6
B_C3 = 4


def width(fields):
    return sum(n for _, n in fields)


def conv_chain(nc, x_in, first_in, second_in, wb_in, out):
    with ExitStack() as ctx:
        def sb(name, shape, dt=F32):
            return ctx.enter_context(nc.sbuf_tensor(name, shape, dt))

        def sem(name):
            return ctx.enter_context(nc.semaphore(name))

        x0 = sb("x0", [P, CT, N])
        x1 = sb("x1", [P, CT, N])
        x2 = sb("x2", [P, CT, N])
        x3 = sb("x3", [P, CT, N])
        yo = sb("yo", [P, CT, N])
        first = sb("first", [P, width(FIRST)])
        second = sb("second", [P, width(SECOND)])
        fld = {}
        for tile, fields in ((first, FIRST), (second, SECOND)):
            at = 0
            for name, n in fields:
                fld[name] = tile[:, at:at + n]
                at += n
        ident = fld["ident"]

        mask_x = sb("mask_x", [P, 8, W])
        mask = sb("mask", [P, N])
        w1bd = sb("w1bd", [P, CT, 2, GROUPS0, G0])
        w2bd = sb("w2bd", [P, TAPSETS, GROUPS0, G0])
        w3bd = sb("w3bd", [HID, GROUPS0, HID])
        pad = sb("pad", [P, PW, PW])
        feat = sb("feat", [HID, N + RUN])
        split = sb("split", [P, PW, PW], F32R)
        offw = [sb(f"offw{b}", [P, TAPS, 4, SLOT], F32R) for b in range(2)]
        om_sb = sb("om_sb", [2 * SLOT, N])
        m0 = sb("m0", [P, N])
        hid = [sb(f"hid{b}", [HID, N]) for b in range(3)]
        feat_t = sb("feat_t", [P, RUN + 1, HID])
        bias_pos = [sb(f"bias_pos{b}", [P, 3, TILES, TAPS]) for b in range(2)]
        pos = sb("pos", [P, 3, TILES * TAPS])
        low = sb("low", [P, 2, TILES * TAPS])
        row_y = sb("row_y", [P, TILES * TAPS])
        dist = sb("dist", [P, 2, TILES * TAPS])
        absd = sb("absd", [P, 2, 2, TILES * TAPS])
        hat = sb("hat", [P, 2, 2, TILES * TAPS])
        sig = sb("sig", [P, TILES * TAPS])
        hat_m = sb("hat_m", [P, 2, TILES * TAPS])
        idx = [sb(f"idx{b}", [P, TILES * TAPS], I32) for b in range(2)]
        G = sb("G", [P, RING, TAPS, PATCH])
        GW = sb("GW", [P, 2, CORNERS, TAPS, HID])
        sT = sb("sT", [P, PAIRS + 1, N])
        st = sb("st", [P, CT, 2, 6])
        mv = sb("mv", [P, CT, 2])
        gm = sb("gm", [P, CT, 2])
        var = sb("var", [P, CT])
        rstd = sb("rstd", [P, CT])
        sc = sb("sc", [P, CT])
        nb = sb("nb", [P, CT])
        zeros = sb("zeros", [TPAD, P])
        half_neg = sb("half_neg", [P, CT])
        pg = sb("pg", [P, TILES, 2 * D])
        th = sb("th", [2 * D, N])
        mt = sb("mt", [D, D])
        at_w = sb("at_w", [D + 1, C])
        ps = ctx.enter_context(nc.psum_tensor("ps", [P, 8, 512], F32))
        table = [nc.dram_tensor(f"table{b}", (TPAD + N, PATCH), F32, kind="Internal").ap()
                 for b in range(2)]

        s_first, s_second, s_wb = sem("s_first"), sem("s_second"), sem("s_wb")
        s_x = [sem(f"s_x{t}") for t in range(CT)]
        s_zero = sem("s_zero")
        s_const = sem("s_const")
        s_mask = sem("s_mask")
        s_wbd = sem("s_wbd")
        s_d = sem("s_d")
        s_c1 = [sem(f"s_c1_{b}") for b in range(3)]
        s_pad = [sem(f"s_pad{b}") for b in range(3)]
        s_hi = [sem(f"s_hi{b}") for b in range(3)]
        s_lo = [sem(f"s_lo{b}") for b in range(3)]
        s_bpos = sem("s_bpos")
        s_offw = sem("s_offw")
        s_omA, s_omD = sem("s_omA"), sem("s_omD")
        s_omc = sem("s_omc")
        s_c2 = [sem(f"s_c2_{b}") for b in range(3)]
        s_hid = [sem(f"s_hid{b}") for b in range(3)]
        s_c3 = [sem(f"s_c3_{b}") for b in range(3)]
        s_t = [sem(f"s_t{b}") for b in range(3)]
        s_xa = [sem(f"s_xa{b}") for b in range(3)]
        s_xd = [sem(f"s_xd{b}") for b in range(3)]
        s_mv = sem("s_mv")
        s_gm = sem("s_gm")
        s_var = sem("s_var")
        s_pow = sem("s_pow")
        s_sb = sem("s_sb")
        s_tr = sem("s_tr")
        s_om = sem("s_om")
        s_ftA, s_ftD = sem("s_ftA"), sem("s_ftD")
        s_tab = [sem(f"s_tab{b}") for b in range(2)]
        s_pos, s_idx, s_dist, s_abs = sem("s_pos"), sem("s_idx"), sem("s_dist"), sem("s_abs")
        s_hat, s_sig, s_w4 = sem("s_hat"), sem("s_sig"), sem("s_w4")
        s_gather = [[sem(f"s_gather{b}_{t}") for t in range(TILES)] for b in range(2)]
        s_gw = sem("s_gw")
        s_st = sem("s_st")
        s_sT = sem("s_sT")
        s_pgm, s_pg = sem("s_pgm"), sem("s_pg")
        s_thm, s_th = sem("s_thm"), sem("s_th")
        s_mtm, s_mt, s_atm, s_at = sem("s_mtm"), sem("s_mt"), sem("s_atm"), sem("s_at")
        s_wy, s_fin, s_yo, s_out = sem("s_wy"), sem("s_fin"), sem("s_yo"), sem("s_out")
        block = ctx.enter_context(nc.Block())

        def half(ap, h):
            return ap[:, h * HALF:(h + 1) * HALF]

        def interior(h, upper):
            p0, r0 = (HID, 0) if upper else (0, 1)
            r0 += h * H // 2
            return pad[p0:p0 + HID, r0:r0 + H // 2, 1:1 + W]

        def half_rows(h):
            return slice(1 + h * H // 2, 1 + (h + 1) * H // 2)

        def as_rows(ap):
            return ap.rearrange("p (y x) -> p y x", x=W)

        def quarter(m, h):
            return ps[:, B_C3 + 2 * m + h, :]

        QUARTERS = [(h, m) for h in range(2) for m in range(CT)]

        def table_view(tab, row, side):
            return tab[row:row + N, side * P:(side + 1) * P].rearrange("(p j) e -> p j e", j=RUN)

        def table_source():
            ap = feat_t[:, 0:RUN, :]
            return bass.AP(ap.tensor, ap.offset, [list(ap.ap[0]), [HID, RUN], [1, 2 * HID]])

        @block.sync
        def _(sp):
            sp.dma_start(first[:], first_in).then_inc(s_first, 16)
            sp.dma_start(x0[:, 1, :], x_in[1]).then_inc(s_x[1], 16)
            sp.dma_start(second[:], second_in).then_inc(s_second, 16)
            sp.dma_start(at_w[D:D + 1, :], wb_in).then_inc(s_wb, 16)
            sp.wait_ge(s_zero, 1)
            for b in range(2):
                sp.dma_start(table[b][0:TPAD, 0:P], zeros[:]).then_inc(s_tab[b], 16)
                sp.dma_start(table[b][N:N + TPAD, P:PATCH], zeros[:]).then_inc(s_tab[b], 16)
            for b in range(2):
                sp.wait_ge(s_ftA, b + 1)
                sp.wait_ge(s_ftD, b + 1)
                sp.dma_start(table_view(table[b], TPAD, 0), table_source()).then_inc(s_tab[b], 16)
            for q, (h, m) in enumerate(QUARTERS):
                if q % 2 == 0:
                    sp.wait_ge(s_yo, q + 1)
                    sp.dma_start(half(out[m], h), half(yo[:, m, :], h)).then_inc(s_out, 16)
            sp.wait_ge(s_out, 16 * len(QUARTERS))

        @block.gpsimd
        def _(pool):
            pool.memset(zeros[:], 0.0).then_inc(s_zero, 1)
            pool.memset(pad[:], 0.0).then_inc(s_const, 1)
            pool.memset(split[:].bitcast(F32), 0.0).then_inc(s_const, 1)
            for b in range(2):
                pool.memset(offw[b][:].bitcast(F32), 0.0).then_inc(s_const, 1)
            pool.memset(feat[:, N:], 0.0).then_inc(s_const, 1)
            pool.memset(half_neg[:], -0.5).then_inc(s_const, 1)
            pool.memset(th[:], 1.0).then_inc(s_const, 1)
            pool.wait_ge(s_first, 16)
            m8 = fld["mask"].rearrange("p (y x) -> p y x", x=8)
            pool.tensor_copy(mask_x[:].rearrange("p y (x r) -> p (y x) r", r=4),
                             fld["mask"][:, :, None].to_broadcast([P, 64, 4])).then_inc(s_mask, 1)
            pool.wait_ge(s_mask, 1)
            pool.tensor_copy(mask[:].rearrange("p (y r x) -> p y r x", r=4, x=W),
                             mask_x[:, :, None, :].to_broadcast([P, 8, 4, W])).then_inc(s_mask, 1)

            def power(norm, p, m):
                pool.wait_ge(s_var, norm)
                pool.tensor_tensor(rstd[0:p, 0:m], var[0:p, 0:m], half_neg[0:p, 0:m],
                                   ALU.pow).then_inc(s_pow, 1)

            def gathers(b):
                pool.wait_ge(s_idx, b + 1)
                pool.wait_ge(s_tab[b], 64)
                for t in range(TILES):
                    done = b * TILES + t
                    if done >= RING:
                        pool.wait_ge(s_gw, done - RING + 1)
                    for k in range(TAPS):
                        n = t * TAPS + k
                        pool.indirect_dma_start(
                            out=G[:, done % RING, k, :], out_offset=None, in_=table[b],
                            in_offset=bass.IndirectOffsetOnAxis(ap=idx[b][:, n:n + 1], axis=0),
                        ).then_inc(s_gather[b][t], 16)

            power(1, HID, 1)
            gathers(0)
            power(2, HID, 1)
            power(3, P, CT)
            gathers(1)
            power(4, P, CT)

        @block.vector
        def _(dve):
            steps = [0]

            def then(ins):
                steps[0] += 1
                ins.then_inc(s_d, 1)
                dve.wait_ge(s_d, steps[0])

            def channel_stats(norm, p, m):
                for i in range(m):
                    then(dve.bn_aggr(mv[0:p, i, :], st[0:p, i, :, :].rearrange("p a b -> p (a b)")))
                for i in range(m):
                    ins = dve.scalar_tensor_tensor(out=mv[0:p, i, 1:2], in0=mv[0:p, i, 0:1],
                                                   scalar=mv[0:p, i, 0:1], in1=mv[0:p, i, 1:2],
                                                   op0=ALU.mult, op1=ALU.add)
                    ins.then_inc(s_mv, 1) if i == m - 1 else then(ins)

            def scale_bias(norm, p, m, stats, gamma, beta):
                dve.wait_ge(s_pow, norm)
                then(dve.tensor_tensor(sc[0:p, 0:m], rstd[0:p, 0:m], gamma, ALU.mult))
                then(dve.tensor_tensor(nb[0:p, 0:m], stats, sc[0:p, 0:m], ALU.mult))
                dve.tensor_tensor(nb[0:p, 0:m], beta, nb[0:p, 0:m], ALU.subtract).then_inc(s_sb, 1)
                dve.wait_ge(s_sb, norm)

            def group_norm(norm, p, m, gamma, beta):
                dve.wait_ge(s_gm, norm)
                then(dve.tensor_copy(gm[0:p, 0:m, :],
                                     ps[0:p, B_OM, 0:2 * m].rearrange("p (m s) -> p m s", s=2)))
                then(dve.tensor_tensor(var[0:p, 0:m], gm[0:p, 0:m, 0], gm[0:p, 0:m, 0], ALU.mult))
                then(dve.tensor_tensor(var[0:p, 0:m], gm[0:p, 0:m, 1], var[0:p, 0:m], ALU.subtract))
                dve.tensor_scalar(var[0:p, 0:m], var[0:p, 0:m], EPS, None, ALU.add).then_inc(s_var, 1)
                scale_bias(norm, p, m, gm[0:p, 0:m, 0], gamma, beta)

            dve.wait_ge(s_first, 16)
            w1c = fld["w1c"].rearrange("p (t o) -> p t o", t=CT)
            w1m = fld["w1m"].rearrange("p (t g) -> p t g", t=CT)
            for twice in range(2):
                dve.tensor_tensor(w1bd[:, :, twice],
                                  w1c[:, :, None, :].to_broadcast([P, CT, GROUPS0, G0]),
                                  w1m[:, :, :, None].to_broadcast([P, CT, GROUPS0, G0]),
                                  ALU.mult).then_inc(s_wbd, 1)
            w2c = fld["w2c"].rearrange("p (t o) -> p t o", t=TAPSETS)
            dve.tensor_tensor(w2bd[:], w2c[:, :, None, :].to_broadcast([P, TAPSETS, GROUPS0, G0]),
                              fld["w2m"][:, None, :, None].to_broadcast([P, TAPSETS, GROUPS0, G0]),
                              ALU.mult).then_inc(s_wbd, 1)
            dve.tensor_tensor(w3bd[:], fld["w3c"][0:HID, None, :].to_broadcast([HID, GROUPS0, HID]),
                              fld["w3m"][0:HID, :, None].to_broadcast([HID, GROUPS0, HID]),
                              ALU.mult).then_inc(s_wbd, 1)

            dve.wait_ge(s_mask, 2)
            dve.wait_ge(s_const, 7)
            for h in range(2):
                dve.wait_ge(s_c1[0], h + 1)
                then(dve.tensor_tensor(half(m0, h), ps[:, B_C1 + h, :], half(mask, h), ALU.mult))
                for upper in range(2):
                    p0 = HID * upper
                    dve.scalar_tensor_tensor(out=interior(h, upper),
                                             in0=as_rows(half(m0[p0:p0 + HID], h)), scalar=0.0,
                                             in1=as_rows(half(mask[p0:p0 + HID], h)),
                                             op0=ALU.max, op1=ALU.mult).then_inc(s_pad[0], 1)
            dve.wait_ge(s_second, 16)
            base = fld["base"].rearrange("p (a t k) -> p a t k", a=3, k=TAPS)
            for b in range(2):
                bo = fld[f"b{b + 1}boff"].rearrange("p (a k) -> p a k", k=TAPS)
                n = (3 - b) * TAPS
                for a in range(3 - b):
                    dve.tensor_tensor(bias_pos[b][:, a], base[:, a],
                                      bo[:, a, None, :].to_broadcast([P, TILES, TAPS]),
                                      ALU.add).then_inc(s_bpos, 1)
                w = fld[f"b{b + 1}off"].rearrange("p (t o) -> p t o", o=n)
                then(dve.tensor_copy(offw[b][:, :, 0, 0:n], w))
                dve.tensor_tensor(offw[b][:, :, 1, 0:n], w, offw[b][:, :, 0, 0:n].bitcast(F32),
                                  ALU.subtract).then_inc(s_offw, 1)
            for h in range(2):
                dve.wait_ge(s_c2[0], h + 1)
                dve.scalar_tensor_tensor(out=half(hid[0], h), in0=ps[0:HID, B_OM + h, :], scalar=0.0,
                                         in1=half(mask[0:HID], h), op0=ALU.max,
                                         op1=ALU.mult).then_inc(s_hid[0], 1)
            for q, (h, m) in enumerate(QUARTERS):
                if m:
                    dve.wait_ge(s_c3[0], q + 1)
                    dve.tensor_scalar(half(x1[:, m, :], h), quarter(m, h), 0.0, None,
                                      ALU.max).then_inc(s_xd[0], 1)

            def split_image(b):
                for h in range(2):
                    rows = slice(1 + h * H // 2, 1 + (h + 1) * H // 2)
                    src = as_rows(half(feat, h))
                    dve.wait_ge(s_pad[b], h + 1)
                    hi = split[0:HID, rows, 1:1 + W]
                    dve.tensor_copy(hi, src).then_inc(s_hi[b], 1)
                    dve.wait_ge(s_hi[b], h + 1)
                    dve.tensor_tensor(split[HID:P, rows, 1:1 + W], src, hi.bitcast(F32),
                                      ALU.subtract).then_inc(s_lo[b], 1)

            def sampling(b):
                axes = 3 - b
                dve.wait_ge(s_tr, b + 1)
                dve.tensor_copy(feat_t[:, RUN, :], ps[:, B_C1 + 1, 0:HID]).then_inc(s_ftD, 1)
                dve.wait_ge(s_omc, 2 * b + 2)
                dve.tensor_copy(half(om_sb, 1), ps[0:2 * SLOT, B_OFF + 1, :]).then_inc(s_omD, 1)
                dve.wait_ge(s_om, b + 1)
                if b:
                    dve.wait_ge(s_w4, 1)
                if not b:
                    dve.wait_ge(s_bpos, 5)
                om = ps[:, B_OM, :].rearrange("p (t s o) -> p t s o", s=2, o=SLOT)
                out_pos = pos[:, 0:axes].rearrange("p a (t k) -> p t a k", k=TAPS)
                for part, other in enumerate((bias_pos[b][:, 0:axes].rearrange("p a t k -> p t a k"),
                                              out_pos)):
                    dve.tensor_tensor(
                        out_pos, om[:, :, part, 0:axes * TAPS].rearrange("p t (a k) -> p t a k", k=TAPS),
                        other, ALU.add).then_inc(s_pos, 1)
                    dve.wait_ge(s_pos, 2 * b + part + 1)
                then(dve.tensor_scalar(low[:], pos[:, 0:2], -0.5, 0.0, ALU.add, ALU.max))
                then(dve.tensor_scalar(low[:], low[:], MAGIC, MAGIC + W - 2, ALU.add, ALU.min))
                then(dve.tensor_scalar(row_y[:], low[:, 1], MAGIC - TPAD // W, float(W), ALU.subtract, ALU.mult))
                dve.scalar_tensor_tensor(out=idx[b][:], in0=low[:, 0], scalar=MAGIC, in1=row_y[:],
                                         op0=ALU.subtract, op1=ALU.add).then_inc(s_idx, 1)
                dve.scalar_tensor_tensor(out=dist[:], in0=low[:], scalar=MAGIC, in1=pos[:, 0:2],
                                         op0=ALU.subtract, op1=ALU.subtract).then_inc(s_dist, 1)
                dve.wait_ge(s_hat, b + 1)
                hy = hat[:, :, 1, :]
                if b == 0:
                    dve.wait_ge(s_sig, 1)
                    then(dve.tensor_tensor(hat_m[:], hat[:, :, 1, :],
                                           sig[:, None, :].to_broadcast([P, 2, TILES * TAPS]), ALU.mult))
                    hy = hat_m[:]
                w4 = ps[:, B_W4, 0:TILES * TAPS * CORNERS].rearrange("p (n y x) -> p n y x", x=2, y=2)
                hx = hat[:, :, 0, :]
                dve.tensor_tensor(
                    w4, hx.rearrange("p r n -> p n r")[:, :, None, :].to_broadcast([P, TILES * TAPS, 2, 2]),
                    hy.rearrange("p r n -> p n r")[:, :, :, None].to_broadcast([P, TILES * TAPS, 2, 2]),
                    ALU.mult).then_inc(s_w4, 1)
                dve.wait_ge(s_w4, b + 1)

            def weigh(b):
                for t in range(TILES):
                    done = b * TILES + t
                    dve.wait_ge(s_gather[b][t], 16 * TAPS)
                    if done >= 2:
                        dve.wait_ge(s_st, done - 1)
                    n = TAPS * CORNERS
                    w = ps[:, B_W4, t * n:(t + 1) * n]
                    dve.tensor_tensor(
                        GW[:, t % 2].rearrange("p c k e -> p k c e"),
                        G[:, done % RING].rearrange("p k (c e) -> p k c e", e=HID),
                        w.rearrange("p (k c) -> p k c", c=CORNERS)[:, :, :, None]
                        .to_broadcast([P, TAPS, CORNERS, HID]), ALU.mult).then_inc(s_gw, 1)

            for h in range(2):
                dve.wait_ge(s_c1[1], h + 1)
                then(dve.bn_stats(st[0:HID, 0, h, :], ps[0:HID, B_C1 + h, :]))
            channel_stats(1, HID, 1)
            group_norm(1, HID, 1, fld["gn1s"][0:HID], fld["gn1b"][0:HID])
            split_image(1)
            sampling(0)
            weigh(0)
            for h in range(2):
                dve.wait_ge(s_c2[1], h + 1)
                then(dve.bn_stats(st[0:HID, 0, h, :], ps[0:HID, B_C1 + h, :]))
            channel_stats(2, HID, 1)
            group_norm(2, HID, 1, fld["gn2s"][0:HID], fld["gn2b"][0:HID])
            for q, (h, m) in enumerate(QUARTERS):
                dve.wait_ge(s_c3[1], q + 1)
                then(dve.bn_stats(st[:, m, h, :], quarter(m, h)))
            channel_stats(3, P, CT)
            group_norm(3, P, CT, fld["gn3s"], fld["gn3b"])
            for h, m in QUARTERS:
                dve.scalar_tensor_tensor(out=half(x2[:, m, :], h), in0=quarter(m, h),
                                         scalar=sc[:, m:m + 1], in1=half(x1[:, m, :], h),
                                         op0=ALU.mult, op1=ALU.add).then_inc(s_t[1], 1)

            split_image(2)
            sampling(1)
            weigh(1)
            for q, (h, m) in enumerate(QUARTERS):
                if m:
                    dve.wait_ge(s_c3[2], q + 1)
                    dve.tensor_scalar(half(x3[:, m, :], h), quarter(m, h), fld["b2b3"][:, m:m + 1], 0.0,
                                      ALU.add, ALU.max).then_inc(s_xd[2], 1)

            dve.wait_ge(s_pgm, 1)
            dve.tensor_tensor(pg[:], ps[:, B_OM, 0:TILES * 2 * D].rearrange("p (t e) -> p t e", e=2 * D),
                              fld["pgb"][:, None, :].to_broadcast([P, TILES, 2 * D]),
                              ALU.add).then_inc(s_pg, 1)
            dve.wait_ge(s_mtm, 1)
            dve.tensor_scalar(mt[:], ps[0:D, B_W4, 0:D], 1.0 / N, None, ALU.mult).then_inc(s_mt, 1)
            dve.wait_ge(s_atm, 1)
            dve.tensor_copy(at_w[0:D, :], ps[0:D, B_W4, 0:C]).then_inc(s_at, 1)
            for q, (h, m) in enumerate(QUARTERS):
                dve.wait_ge(s_wy, q + 1)
                then(dve.bn_stats(st[:, m, h, :], quarter(m, h)))
            for m in range(CT):
                then(dve.bn_aggr(mv[:, m, :], st[:, m, :, :].rearrange("p a b -> p (a b)")))
            dve.tensor_scalar(var[:], mv[:, :, 1], EPS, None, ALU.add).then_inc(s_var, 1)
            scale_bias(4, P, CT, mv[:, :, 0], fld["bns"], fld["bnb"])
            for q, (h, m) in enumerate(QUARTERS):
                dve.wait_ge(s_fin, q + 1)
                dve.tensor_tensor(half(yo[:, m, :], h), half(yo[:, m, :], h), half(x3[:, m, :], h),
                                  ALU.add).then_inc(s_yo, 1)

        @block.scalar
        def _(act):
            act.dma_start(x0[:, 0, :], x_in[0]).then_inc(s_x[0], 16)
            for q, (h, m) in enumerate(QUARTERS):
                if not m:
                    act.wait_ge(s_c3[0], q + 1)
                    act.activation(half(x1[:, m, :], h), quarter(m, h), ACT.Relu).then_inc(s_xa[0], 1)

            def features(b, scale, bias):
                for h in range(2):
                    act.activation(half(feat, h), ps[0:HID, B_C1 + h, :], ACT.Relu,
                                   scale=scale, bias=bias).then_inc(s_pad[b], 1)

            def sampling(b):
                act.wait_ge(s_tr, b + 1)
                act.activation(feat_t[:, 0:RUN, :], ps[:, B_C1, :].rearrange("p (j e) -> p j e", e=HID),
                               ACT.Copy).then_inc(s_ftA, 1)
                act.wait_ge(s_ftA, b + 1)
                act.wait_ge(s_ftD, b + 1)
                act.dma_start(table_view(table[b], 0, 1), table_source()).then_inc(s_tab[b], 16)
                act.wait_ge(s_omc, 2 * b + 1)
                act.activation(half(om_sb, 0), ps[0:2 * SLOT, B_OFF, :], ACT.Copy).then_inc(s_omA, 1)
                if b == 0:
                    act.wait_ge(s_pos, 2)
                    act.activation(sig[:], pos[:, 2], ACT.Sigmoid).then_inc(s_sig, 1)
                act.wait_ge(s_dist, b + 1)
                for r in range(2):
                    act.activation(absd[:, r], dist[:], ACT.Abs, bias=float(r)).then_inc(s_abs, 1)
                act.wait_ge(s_abs, 2 * b + 2)
                act.activation(hat[:], absd[:], ACT.Relu, scale=-1.0, bias=1.0).then_inc(s_hat, 1)

            def samples(b):
                for t in range(TILES):
                    done = b * TILES + t
                    act.wait_ge(s_st, done + 1)
                    act.activation(sT[:, 0:PAIRS, t * P:(t + 1) * P],
                                   ps[:, B_ST + t % 2, :].rearrange("p (q n) -> p q n", n=P),
                                   ACT.Copy).then_inc(s_sT, 1)
                    act.activation(sT[0:HID, PAIRS, t * P:(t + 1) * P], ps[0:HID, B_ST1 + t % 2, 0:P],
                                   ACT.Copy).then_inc(s_sT, 1)

            act.wait_ge(s_sb, 1)
            features(1, sc[0:HID, 0:1], nb[0:HID, 0:1])
            sampling(0)
            samples(0)
            act.wait_ge(s_sb, 2)
            for h in range(2):
                act.activation(half(hid[1], h), ps[0:HID, B_C1 + h, :], ACT.Relu,
                               scale=sc[0:HID, 0:1], bias=nb[0:HID, 0:1]).then_inc(s_hid[1], 1)
            for q, (h, m) in enumerate(QUARTERS):
                act.wait_ge(s_t[1], q + 1)
                act.activation(half(x2[:, m, :], h), half(x2[:, m, :], h), ACT.Relu,
                               bias=nb[:, m:m + 1]).then_inc(s_xa[1], 1)

            act.wait_ge(s_c1[2], 2)
            features(2, 1.0, fld["b2b1"][0:HID])
            sampling(1)
            samples(1)
            for h in range(2):
                act.wait_ge(s_c2[2], h + 1)
                act.activation(half(hid[2], h), ps[0:HID, B_C1 + h, :], ACT.Relu,
                               bias=fld["b2b2"][0:HID]).then_inc(s_hid[2], 1)
            for q, (h, m) in enumerate(QUARTERS):
                if not m:
                    act.wait_ge(s_c3[2], q + 1)
                    act.activation(half(x3[:, m, :], h), quarter(m, h), ACT.Relu,
                                   bias=fld["b2b3"][:, m:m + 1]).then_inc(s_xa[2], 1)

            for h in range(2):
                act.wait_ge(s_thm, h + 1)
                act.activation(half(th[0:D], h), ps[0:D, B_C1 + h, :], ACT.Identity,
                               bias=fld["thb"][0:D]).then_inc(s_th, 1)
            act.wait_ge(s_sb, 4)
            for q, (h, m) in enumerate(QUARTERS):
                act.activation(half(yo[:, m, :], h), quarter(m, h), ACT.Identity,
                               scale=sc[:, m:m + 1], bias=nb[:, m:m + 1]).then_inc(s_fin, 1)
                if q % 2:
                    act.wait_ge(s_yo, q + 1)
                    act.dma_start(half(out[m], h), half(yo[:, m, :], h)).then_inc(s_out, 16)

        @block.tensor
        def _(pe):
            def conv1(b, weights, src):
                m = weights.shape[2]
                for h in range(2):
                    for t in range(CT):
                        mm = pe.matmul(ps[0:m, B_C1 + h, :], weights[:, t, :], half(src[:, t, :], h),
                                       start=(t == 0), stop=(t == CT - 1))
                    mm.then_inc(s_c1[b], 1)

            def tapsets():
                return [(P, 0, kx) for kx in range(3)] + [(HID, 2, kx) for kx in range(3)]

            def residual(src):
                for h, m in QUARTERS:
                    pe.matmul(quarter(m, h), ident, half(src[:, m, :], h), start=True, stop=False)

            def conv3(b, weights, start):
                for h in range(2):
                    pe.wait_ge(s_hid[b], h + 1)
                    for m in range(CT):
                        pe.matmul(quarter(m, h), weights[:, m * P:(m + 1) * P], half(hid[b], h),
                                  start=start, stop=True).then_inc(s_c3[b], 1)

            def group_stats(norm, p, m, matrix):
                pe.wait_ge(s_mv, norm)
                pe.matmul(ps[0:p, B_OM, 0:2 * m], matrix[0:p, 0:p],
                          mv[0:p, 0:m, :].rearrange("p m s -> p (m s)"),
                          start=True, stop=True).then_inc(s_gm, 1)

            def features(b):
                pe.wait_ge(s_pad[b + 1], 2)
                for j in range(RUN + 1):
                    tr = pe.transpose(ps[:, B_C1 + j // RUN, (j % RUN) * HID:(j % RUN + 1) * HID],
                                      feat[:, j:j + (P - 1) * RUN + 1:RUN], ident[0:HID, 0:HID])
                tr.then_inc(s_tr, 1)
                pe.wait_ge(s_offw, b + 1)
                pe.wait_ge(s_lo[b + 1], 2)
                for h in range(2):
                    for k in range(TAPS):
                        r = h * H // 2 + k // 3
                        om = pe.matmul(ps[:, B_OFF + h, :],
                                       offw[b][:, k].rearrange("p s o -> p (s o)"),
                                       split[:, r:r + H // 2, k % 3:k % 3 + W],
                                       start=(k == 0), stop=(k == TAPS - 1))
                    om.then_inc(s_omc, 1)
                for t in range(TILES):
                    if t == 0:
                        pe.wait_ge(s_omA, b + 1)
                    if t == TILES // 2:
                        pe.wait_ge(s_omD, b + 1)
                    om = pe.transpose(ps[:, B_OM, t * 2 * SLOT:(t + 1) * 2 * SLOT],
                                      om_sb[:, t * P:(t + 1) * P], ident[0:2 * SLOT, 0:2 * SLOT])
                om.then_inc(s_om, 1)

            def deform(b, weights):
                w = weights.rearrange("p (q o) -> p q o", o=HID)

                def contract(t):
                    pe.wait_ge(s_sT, 2 * (b * TILES + t + 1))
                    for q in range(PAIRS + 1):
                        p = P if q < PAIRS else HID
                        mm = pe.matmul(ps[0:HID, B_C1 + t // 4, t % 4 * P:(t % 4 + 1) * P], w[0:p, q, :],
                                       sT[0:p, q, t * P:(t + 1) * P], start=(q == 0), stop=(q == PAIRS))
                    if t % 4 == 3:
                        mm.then_inc(s_c2[b + 1], 1)

                for t in range(TILES):
                    done = b * TILES + t
                    pe.wait_ge(s_gw, done + 1)
                    if done >= 2:
                        pe.wait_ge(s_sT, 2 * (done - 1))
                    for q in range(PAIRS + 1):
                        k = 2 * q
                        n = min(2, TAPS - k)
                        dst = ps[:, B_ST + t % 2, q * P:(q + 1) * P] if n == 2 else ps[0:HID, B_ST1 + t % 2, 0:P]
                        for c in range(CORNERS):
                            mm = pe.matmul(dst, GW[:, t % 2, c, k:k + n, :].rearrange("p k e -> p (k e)"),
                                           ident, is_transpose=True, start=(c == 0), stop=(c == CORNERS - 1))
                    mm.then_inc(s_st, 1)
                    if t:
                        contract(t - 1)
                contract(TILES - 1)

            pe.wait_ge(s_wbd, 4)
            for t in range(CT):
                pe.wait_ge(s_x[t], 16)
            conv1(0, w1bd[:].rearrange("p t d g o -> p t (d g o)"), x0)
            residual(x0)
            pe.wait_ge(s_pad[0], 4)
            for h in range(2):
                for e, (p, r, kx) in enumerate(tapsets()):
                    r0 = r + h * H // 2
                    mm = pe.matmul(ps[0:HID, B_OM + h, :], w2bd[0:p, e].rearrange("p g o -> p (g o)"),
                                   pad[0:p, r0:r0 + H // 2, kx:kx + W],
                                   start=(e == 0), stop=(e == TAPSETS - 1))
                mm.then_inc(s_c2[0], 1)
            conv3(0, w3bd[:].rearrange("p g o -> p (g o)"), False)

            pe.wait_ge(s_xa[0], 2)
            pe.wait_ge(s_xd[0], 2)
            pe.wait_ge(s_second, 16)
            conv1(1, fld["b1w1"].rearrange("p (t o) -> p t o", o=HID), x1)
            group_stats(1, HID, 1, fld["g2"])
            features(0)
            deform(0, fld["b1w2"])
            group_stats(2, HID, 1, fld["g2"])
            conv3(1, fld["b1w3"][0:HID], True)
            group_stats(3, P, CT, fld["g8"])

            pe.wait_ge(s_xa[1], 4)
            conv1(2, fld["b2w1"].rearrange("p (t o) -> p t o", o=HID), x2)
            features(1)
            deform(1, fld["b2w2"])
            residual(x2)
            conv3(2, fld["b2w3"][0:HID], False)

            pgw = fld["pgw"].rearrange("p (t e) -> p t e", e=2 * D)
            thw = fld["thw"].rearrange("p (t e) -> p t e", e=D)
            for h in range(2):
                pe.wait_ge(s_xa[2], h + 1)
                pe.wait_ge(s_xd[2], h + 1)
                for t in range(h * TILES // 2, (h + 1) * TILES // 2):
                    for i in range(CT):
                        mm = pe.matmul(ps[:, B_OM, t * 2 * D:(t + 1) * 2 * D],
                                       x3[:, i, t * P:(t + 1) * P], pgw[:, i, :],
                                       start=(i == 0), stop=(i == CT - 1))
                if h:
                    mm.then_inc(s_pgm, 1)
                for i in range(CT):
                    mm = pe.matmul(ps[0:D, B_C1 + h, :], thw[:, i, :], half(x3[:, i, :], h),
                                   start=(i == 0), stop=(i == CT - 1))
                mm.then_inc(s_thm, 1)
            pe.wait_ge(s_pg, 1)
            for t in range(TILES):
                mm = pe.matmul(ps[0:D, B_W4, 0:D], pg[:, t, D:2 * D], pg[:, t, 0:D],
                               start=(t == 0), stop=(t == TILES - 1))
            mm.then_inc(s_mtm, 1)
            pe.wait_ge(s_mt, 1)
            pe.matmul(ps[0:D, B_W4, 0:C], mt[:], fld["www"][0:D], start=True, stop=True).then_inc(s_atm, 1)
            pe.wait_ge(s_at, 1)
            pe.wait_ge(s_wb, 16)
            pe.wait_ge(s_th, 2)
            for h, m in QUARTERS:
                pe.matmul(quarter(m, h), at_w[:, m * P:(m + 1) * P], half(th[0:D + 1], h),
                          start=True, stop=True).then_inc(s_wy, 1)


def constants():
    import numpy as np

    p = np.arange(P)
    w1m = np.zeros((P, CT, GROUPS0), np.float32)
    for t in range(CT):
        w1m[p, t, 2 * t + p // HID] = 1
    wm = np.zeros((P, GROUPS0), np.float32)
    wm[p, p % HID // G0] = 1
    k = np.arange(TAPS)
    base = np.zeros((P, 3, TILES, TAPS), np.float32)
    t = np.arange(TILES)[None, :, None]
    base[:, 0] = (p % W)[:, None, None] + k % 3 - 1 + 0 * t
    base[:, 1] = (p // W)[:, None, None] + ROWS * t + k // 3 - 1
    return {"w1m": w1m, "w2m": wm, "w3m": wm, "ident": np.eye(P, dtype=np.float32),
            "g2": np.kron(np.eye(P // 2), np.full((2, 2), 1 / 2)).astype(np.float32),
            "g8": np.kron(np.eye(P // 8), np.full((8, 8), 1 / 8)).astype(np.float32),
            "base": base}


def pack(fields, parts):
    import numpy as np

    packed = np.zeros((P, width(fields)), np.float32)
    at = 0
    for name, n in fields:
        a = parts[name]
        a = a.reshape(a.shape[0], -1)
        packed[:a.shape[0], at:at + a.shape[1]] = a
        at += n
    return packed


def lay_out(i):
    import numpy as np

    def col(v):
        return v.reshape(-1, P).T

    def twice(v):
        return np.concatenate([v, v]).reshape(P, 1)

    def tapsets(w):
        top = w[:, :, 0, :].transpose(1, 2, 0)
        mid = w[:, :, 1, :].transpose(1, 2, 0)
        low = w[:, :, 2, :].transpose(1, 2, 0)
        return np.concatenate([np.concatenate([top, low], 1), np.concatenate([mid, np.zeros_like(low)], 1)], 0)

    def taps(w):
        return np.tile(w.reshape(w.shape[0], HID, TAPS).transpose(1, 2, 0), (2, 1, 1))

    def channels(w):
        return w.reshape(w.shape[0], CT, P).transpose(2, 1, 0)

    def pairs(w):
        w = w.reshape(HID, HID, TAPS).transpose(2, 1, 0)
        w = np.concatenate([w, np.zeros_like(w[:1])], 0)
        return w.reshape(PAIRS + 1, P, HID).transpose(1, 0, 2)

    def rows(v):
        return np.broadcast_to(v.reshape(1, -1), (P, v.size))

    xy = [2 * k + 1 for k in range(TAPS)] + [2 * k for k in range(TAPS)]
    w1 = i["L0_conv_w1"].reshape(CT, 2, G0, HID).transpose(1, 3, 0, 2).reshape(P, CT * G0)
    m = i["L0_conv_mask"].reshape(GROUPS0, 64)
    w3 = i["L0_conv_w3"].reshape(GROUPS0, HID, G0).transpose(0, 2, 1).reshape(HID, HID)
    w2 = tapsets(i["L0_conv_w2"].reshape(GROUPS0, G0, G0, 3, 3).transpose(1, 0, 2, 3, 4)
                 .reshape(G0, HID, 3, 3))
    parts = dict(constants())
    parts.update({
        "w1c": w1, "mask": np.tile(np.repeat(m, G0, 0), (2, 1)), "w2c": w2, "w3c": w3,
        "b1w1": channels(i["L1_conv_w1"].reshape(HID, C)), "b1off": taps(i["L1_conv_w_off"]),
        "b1boff": rows(i["L1_conv_b_off"]), "b1w2": pairs(i["L1_conv_w2"]),
        "b1w3": i["L1_conv_w3"].reshape(C, HID).T,
        "gn1s": twice(i["L1_conv_gn1_scale"]), "gn1b": twice(i["L1_conv_gn1_bias"]),
        "gn2s": twice(i["L1_conv_gn2_scale"]), "gn2b": twice(i["L1_conv_gn2_bias"]),
        "gn3s": col(i["L1_conv_gn3_scale"]), "gn3b": col(i["L1_conv_gn3_bias"]),
        "b2w1": channels(i["L2_conv_w1"].reshape(HID, C)), "b2off": taps(i["L2_conv_w_off"][xy]),
        "b2boff": rows(i["L2_conv_b_off"][xy]), "b2w2": pairs(i["L2_conv_w2"]),
        "b2w3": i["L2_conv_w3"].reshape(C, HID).T,
        "b2b1": twice(i["L2_conv_b1"]), "b2b2": twice(i["L2_conv_b2"]), "b2b3": col(i["L2_conv_b3"]),
        "pgw": channels(np.concatenate([i["L3_conv_phi_w"], i["L3_conv_g_w"]])),
        "pgb": rows(np.concatenate([i["L3_conv_phi_b"], i["L3_conv_g_b"]])),
        "thw": channels(i["L3_conv_theta_w"]), "thb": i["L3_conv_theta_b"].reshape(D, 1),
        "www": i["L3_conv_w_w"].T, "bns": col(i["L3_conv_bn_gamma"]), "bnb": col(i["L3_conv_bn_beta"]),
    })
    return {"x": i["x"].reshape(CT, P, N), "first": pack(FIRST, parts), "second": pack(SECOND, parts),
            "w_b": i["L3_conv_w_b"].reshape(1, C)}


def kernel(**inputs):
    import numpy as np
    import concourse.bacc as bacc
    from concourse.bass_utils import run_bass_kernel_spmd as run

    arrays = {f"in_{k}": np.ascontiguousarray(v)
              for k, v in lay_out({k: np.asarray(v) for k, v in inputs.items()}).items()}
    nc = bacc.Bacc("TRN2", target_bir_lowering=False, num_devices=1)
    args = [nc.dram_tensor(k, a.shape, mybir.dt.from_np(a.dtype), kind="ExternalInput").ap()
            for k, a in arrays.items()]
    out = nc.dram_tensor("out", (CT, P, N), F32, kind="ExternalOutput").ap()
    conv_chain(nc, *args, out)
    r = run(nc, [arrays], core_ids=[0])
    return r.results[0]["out"].reshape(1, C, H, W)
```

```python
from contextlib import ExitStack

import concourse.bass as bass
from concourse import mybir

F32 = mybir.dt.float32
F32R = mybir.dt.float32r
I32 = mybir.dt.int32
ALU = mybir.AluOpType
ACT = mybir.ActivationFunctionType

P = 128
C = 256
CT = C // P
H = W = 32
N = H * W
HALF = N // 2
TILES = N // P
ROWS = P // W
HID = 64
TAPS = 9
DENSE = 2
GTAPS = TAPS - DENSE
PAIRS = GTAPS // 2
CHUNKS = DENSE * TILES
PARTS = [(0, 4), (4, GTAPS)]
UNITS = len(PARTS) * TILES
IDLE = [13, 6, 14, 8, 12, 8, 10, 2, 6, 2, 4, 2, 3, 3, 1, 1]
LAG = 2
BESIDE = [0, 0, 1, 1, 2, 1, 1, 2, 1, 1, 2, 1, 1, 2, 0, 0]
RESIDUAL = [1, 0, 1, 2]
AHEAD = 2
FIRST_TAP_ENDS = [sum(BESIDE[:u + 1]) >= TILES for u in range(UNITS)].index(True)
PREPARE = [(-1, -1, -1), (3, FIRST_TAP_ENDS - AHEAD, 5)]
HRING = 3
SRING = 4
CORNERS = 4
PATCH = CORNERS * HID
PW = W + 2
GROUPS0 = 4
G0 = HID // GROUPS0
D = 16
EPS = 1e-5
MAGIC = 1.5 * 2.0 ** 23
SLOT = 32
RUN = N // P
RING = 5
TPAD = H

FIRST = [("w1c", CT * G0), ("w1m", CT * GROUPS0), ("mask", 64), ("w2c", TAPS * G0),
         ("w2m", GROUPS0), ("w3c", HID), ("w3m", GROUPS0), ("ident", P)]
SECOND = [("g2", P), ("g8", P), ("base", 3 * TILES * TAPS), ("dbase", 3 * CHUNKS), ("sel", 3 * DENSE), ("ramp", W + P),
          ("b1w1", CT * HID), ("b1off", TAPS * 27), ("b1boff", 27), ("b1w2", (PAIRS + 1) * HID), ("b1wd", DENSE * HID), ("b1w3", C),
          ("gn1s", 1), ("gn1b", 1), ("gn2s", 1), ("gn2b", 1), ("gn3s", CT), ("gn3b", CT),
          ("b2w1", CT * HID), ("b2off", TAPS * 18), ("b2boff", 18), ("b2w2", (PAIRS + 1) * HID), ("b2wd", DENSE * HID), ("b2w3", C),
          ("b2b1", 1), ("b2b2", 1), ("b2b3", CT),
          ("tpgw", CT * 4 * D), ("pgb", 2 * D), ("thb", 1), ("www", C),
          ("bns", CT), ("bnb", CT)]

B_C1 = 0
B_OM = 2
B_ST = [2, 3]
B_SMALL = 3
B_OFF = 4
B_V = 0
B_D = [4, 5]
B_Y = 6
B_C3 = 4


def width(fields):
    return sum(n for _, n in fields)


def conv_chain(nc, x_in, first_in, second_in, wb_in, out):
    with ExitStack() as ctx:
        def sb(name, shape, dt=F32):
            return ctx.enter_context(nc.sbuf_tensor(name, shape, dt))

        def sem(name):
            return ctx.enter_context(nc.semaphore(name))

        x0 = sb("x0", [P, CT, N])
        x1 = sb("x1", [P, CT, N])
        x2 = sb("x2", [P, CT, N])
        x3 = x1
        yo = x0
        first = sb("first", [P, width(FIRST)])
        second = sb("second", [P, width(SECOND)])
        fld = {}
        for tile, fields in ((first, FIRST), (second, SECOND)):
            at = 0
            for name, n in fields:
                fld[name] = tile[:, at:at + n]
                at += n
        ident = fld["ident"]

        mask_x = sb("mask_x", [HID, 8, W])
        mask = sb("mask", [P, N])
        w1bd = sb("w1bd", [P, CT, GROUPS0, G0])
        w2s = sb("w2s", [P, TAPS, 2, HID], F32R)
        w3bd = sb("w3bd", [HID, GROUPS0, HID])
        feat = sb("feat", [HID, N + RUN])
        split = sb("split", [P, PW, PW], F32R)
        offw = [sb(f"offw{b}", [P, TAPS, 4, SLOT], F32R) for b in range(2)]
        om_sb = sb("om_sb", [2 * SLOT, N])
        om_split = sb("om_split", [P, N], F32R)
        m0 = sb("m0", [P, N])
        hid = 3 * [sb("hid", [HID, N])]
        feat_t = sb("feat_t", [P, RUN + 1, HID])
        bias_pos = [sb(f"bias_pos{b}", [P, 3, TILES, TAPS]) for b in range(2)]
        pos = sb("pos", [P, 3, TILES * TAPS])
        low = sb("low", [P, 2, TILES * TAPS])
        row_y = sb("row_y", [P, TILES * TAPS])
        dist = sb("dist", [P, 2, TILES * TAPS])
        absd = sb("absd", [P, 2, 2, TILES * TAPS])
        hat = sb("hat", [P, 2, 2, TILES * TAPS])
        sig = sb("sig", [P, TILES * TAPS])
        corner_w = sb("corner_w", [P, TILES * TAPS * CORNERS])
        hat_m = sb("hat_m", [P, 2, TILES * TAPS])
        idx = [sb(f"idx{b}", [P, TILES * TAPS], I32) for b in range(2)]
        G = sb("G", [P, RING, GTAPS, PATCH])
        GW = sb("GW", [P, CORNERS, GTAPS, HID])
        GA = sb("GA", [P, 2, GTAPS, HID])
        GS = sb("GS", [P, 2, GTAPS, HID])
        dbias = [sb(f"dbias{b}", [P, 3, DENSE, TILES]) for b in range(2)]
        sel = sb("sel", [P, DENSE, 3, P], F32R)
        ramp = sb("ramp", [1, W + P], F32R)
        V = sb("V", [P, TILES, DENSE, HID])
        near_x = sb("near_x", [P, N])
        w2bd = (near_x[:, 0:TAPS * HID]
                .rearrange("p (t g o) -> p t g o", t=TAPS, g=GROUPS0))
        hat_x = sb("hat_x", [P, DENSE, N])
        mod_x = m0
        near_y = sb("near_y", [P, 2, N])
        hat_y_ring = sb("hat_y", [P, HRING, N])
        hat_y = [hat_y_ring[:, n] for n in range(HRING)]
        S_own = sb("S", [P, N])
        S = [S_own[:], x0[:, 0, :], x0[:, 1, :], mask[:]]
        sT = sb("sT", [P, 2, PAIRS + 1, P])
        st = sb("st", [P, CT, 2, 6])
        mv = sb("mv", [P, CT, 2])
        gm = sb("gm", [P, CT, 2])
        var = sb("var", [P, CT])
        rstd = sb("rstd", [P, CT])
        sc = sb("sc", [P, CT])
        nb = sb("nb", [P, CT])
        zeros = sb("zeros", [P, P])
        warm = sb("warm", [TPAD, 1])
        half_neg = sb("half_neg", [P, CT])
        pgT = feat[0:2 * D]
        pg = sb("pg", [P, TILES, 2 * D])
        th = sb("th", [2 * D, N])
        mt = sb("mt", [D, D])
        at_w = sb("at_w", [D + 1, C])
        ps = ctx.enter_context(nc.psum_tensor("ps", [P, 8, 512], F32))
        table = [nc.dram_tensor(f"table{b}", (TPAD + N, PATCH), F32, kind="Internal").ap()
                 for b in range(2)]

        s_first, s_second, s_wb = sem("s_first"), sem("s_second"), sem("s_wb")
        s_x = [sem(f"s_x{t}") for t in range(CT)]
        s_zero = sem("s_zero")
        s_const = sem("s_const")
        s_wbd = sem("s_wbd")
        s_masked = sem("s_masked")
        s_low = sem("s_low")
        s_d = sem("s_d")
        s_c1 = [sem(f"s_c1_{b}") for b in range(3)]
        s_pad = [sem(f"s_pad{b}") for b in range(3)]
        s_hi = [sem(f"s_hi{b}") for b in range(3)]
        s_lo = [sem(f"s_lo{b}") for b in range(3)]
        s_bpos = sem("s_bpos")
        s_offw = sem("s_offw")
        s_omA = sem("s_omA")
        s_omc = sem("s_omc")
        s_c2 = [sem(f"s_c2_{b}") for b in range(3)]
        s_hid = [sem(f"s_hid{b}") for b in range(3)]
        s_c3 = [sem(f"s_c3_{b}") for b in range(3)]
        s_t = [sem(f"s_t{b}") for b in range(3)]
        s_xa = [sem(f"s_xa{b}") for b in range(3)]
        s_xd = [sem(f"s_xd{b}") for b in range(3)]
        s_mv = sem("s_mv")
        s_gm = sem("s_gm")
        s_var = sem("s_var")
        s_pow = sem("s_pow")
        s_sb = sem("s_sb")
        s_tr = sem("s_tr")
        s_om = sem("s_om")
        s_ftA, s_ftD = sem("s_ftA"), sem("s_ftD")
        s_tab = [sem(f"s_tab{b}") for b in range(2)]
        s_pos, s_idx, s_dist, s_abs = sem("s_pos"), sem("s_idx"), sem("s_dist"), sem("s_abs")
        s_hat, s_sig, s_w4 = sem("s_hat"), sem("s_sig"), sem("s_w4")
        s_gather = [[[sem(f"s_gather{b}_{t}_{part}") for part in range(len(PARTS))]
                     for t in range(TILES)] for b in range(2)]
        s_gw = sem("s_gw")
        s_ga = sem("s_ga")
        s_gs = sem("s_gs")
        s_sel = sem("s_sel")
        s_omhi, s_omlo = sem("s_omhi"), sem("s_omlo")
        s_dbias = sem("s_dbias")
        s_V = sem("s_V")
        s_full = [sem(f"s_full{n}") for n in range(len(B_D))]
        s_free = [sem(f"s_free{n}") for n in range(len(B_D))]
        s_y = sem("s_y")
        s_nx = sem("s_nx")
        s_hx = sem("s_hx")
        s_hxm = sem("s_hxm")
        s_ny = sem("s_ny")
        s_hy = sem("s_hy")
        s_S = sem("s_S")
        s_dense = sem("s_dense")
        s_st = sem("s_st")
        s_sT = sem("s_sT")
        s_pgm, s_pg = sem("s_pgm"), sem("s_pg")
        s_tpg = sem("s_tpg")
        s_th, s_pgT = sem("s_th"), sem("s_pgT")
        s_mtm, s_mt, s_atm, s_at = sem("s_mtm"), sem("s_mt"), sem("s_atm"), sem("s_at")
        s_wy, s_out = sem("s_wy"), sem("s_out")
        s_finA, s_finD = sem("s_finA"), sem("s_finD")
        s_yo = [sem(f"s_yo{m}") for m in range(CT)]
        block = ctx.enter_context(nc.Block())

        def half(ap, h):
            return ap[:, h * HALF:(h + 1) * HALF]

        def half_rows(h):
            return slice(1 + h * H // 2, 1 + (h + 1) * H // 2)

        def as_rows(ap):
            return ap.rearrange("p (y x) -> p y x", x=W)

        def quarter(m, h):
            return ps[:, B_C3 + 2 * m + h, :]

        def chunks_at(u):
            return range(sum(BESIDE[:u]), sum(BESIDE[:u + 1]))

        def prepared_at(u, b):
            return [(i, axis) for i in range(DENSE) for axis in range(3 - b)
                    if PREPARE[i][axis] == u]

        QUARTERS = [(h, m) for h in range(2) for m in range(CT)]
        LAST_QUARTERS = [(0, 1), (0, 0), (1, 0), (1, 1)]

        order = [(b, i, axis, h) for b in range(2) for i in range(DENSE)
                 for axis in range(0, 3 - b, 2) for h in range(2)]

        def turn(*which):
            return order.index(which) % len(B_D), order.index(which) // len(B_D)

        def table_view(tab, row, side):
            return tab[row:row + N, side * P:(side + 1) * P].rearrange("(p j) e -> p j e", j=RUN)

        def table_source():
            ap = feat_t[:, 0:RUN, :]
            return bass.AP(ap.tensor, ap.offset, [list(ap.ap[0]), [HID, RUN], [1, 2 * HID]])

        @block.sync
        def _(sp):
            sp.dma_start(first[:], first_in).then_inc(s_first, 16)
            sp.dma_start(x0[:, 1, :], x_in[1]).then_inc(s_x[1], 16)
            sp.dma_start(second[:], second_in).then_inc(s_second, 16)
            sp.dma_start(at_w[D:D + 1, :], wb_in).then_inc(s_wb, 16)
            sp.wait_ge(s_zero, 1)
            for b in range(2):
                sp.dma_start(table[b][0:TPAD, 0:P], zeros[0:TPAD]).then_inc(s_tab[b], 16)
                sp.dma_start(table[b][N:N + TPAD, P:PATCH], zeros[0:TPAD]).then_inc(s_tab[b], 16)
            for b in range(2):
                sp.wait_ge(s_ftA, b + 1)
                sp.wait_ge(s_ftD, b + 1)
                sp.dma_start(table_view(table[b], TPAD, 0), table_source()).then_inc(s_tab[b], 16)
            for h, m in QUARTERS:
                sp.wait_ge(s_yo[m], h + 1)
                sp.dma_start(half(out[m], h), half(yo[:, m, :], h)).then_inc(s_out, 16)
            sp.wait_ge(s_out, 16 * len(QUARTERS))

        @block.gpsimd
        def _(pool):
            pool.memset(zeros[:], 0.0).then_inc(s_zero, 1)
            pool.memset(split[:].bitcast(F32), 0.0).then_inc(s_const, 1)
            for b in range(2):
                pool.memset(offw[b][:].bitcast(F32), 0.0).then_inc(s_const, 1)
            pool.memset(feat[:, N:], 0.0).then_inc(s_const, 1)
            pool.memset(half_neg[:], -0.5).then_inc(s_const, 1)
            pool.memset(th[:], 1.0).then_inc(s_const, 1)
            def power(norm, p, m):
                pool.wait_ge(s_var, norm)
                pool.tensor_tensor(rstd[0:p, 0:m], var[0:p, 0:m], half_neg[0:p, 0:m],
                                   ALU.pow).then_inc(s_pow, 1)

            def gathers(b):
                pool.wait_ge(s_tab[b], 64)
                for t in range(TILES):
                    done = b * TILES + t
                    if t % (TILES // 2) == 0:
                        pool.wait_ge(s_idx, 2 * b + t // (TILES // 2) + 1)
                    if done >= RING:
                        pool.wait_ge(s_gw, len(PARTS) * (done - RING + 1))
                    for k in range(GTAPS):
                        n = t * TAPS + k
                        pool.indirect_dma_start(
                            out=G[:, done % RING, k, :], out_offset=None, in_=table[b],
                            in_offset=bass.IndirectOffsetOnAxis(ap=idx[b][:, n:n + 1], axis=0),
                        ).then_inc(s_gather[b][t][int(k >= PARTS[1][0])], 16)

            power(1, HID, 1)
            gathers(0)
            power(2, HID, 1)
            power(3, P, CT)
            gathers(1)
            power(4, P, CT)

        @block.vector
        def _(dve):
            steps = [0]
            bias_steps = [0]

            def then(ins):
                steps[0] += 1
                ins.then_inc(s_d, 1)
                dve.wait_ge(s_d, steps[0])

            def channel_stats(norm, p, m):
                for i in range(m):
                    then(dve.bn_aggr(mv[0:p, i, :], st[0:p, i, :, :].rearrange("p a b -> p (a b)")))
                for i in range(m):
                    ins = dve.scalar_tensor_tensor(out=mv[0:p, i, 1:2], in0=mv[0:p, i, 0:1],
                                                   scalar=mv[0:p, i, 0:1], in1=mv[0:p, i, 1:2],
                                                   op0=ALU.mult, op1=ALU.add)
                    ins.then_inc(s_mv, 1) if i == m - 1 else then(ins)

            def scale_bias(norm, p, m, mean, gamma, beta):
                then(dve.tensor_scalar(nb[0:p, 0:m], mean, -1.0, None, ALU.mult))
                dve.wait_ge(s_pow, norm)
                then(dve.tensor_tensor(sc[0:p, 0:m], rstd[0:p, 0:m], gamma, ALU.mult))
                for i in range(m):
                    dve.scalar_tensor_tensor(out=nb[0:p, i:i + 1], in0=nb[0:p, i:i + 1],
                                             scalar=sc[0:p, i:i + 1], in1=beta[:, i:i + 1],
                                             op0=ALU.mult, op1=ALU.add).then_inc(s_sb, 1)
                bias_steps[0] += m
                dve.wait_ge(s_sb, bias_steps[0])

            def group_norm(norm, p, m, gamma, beta):
                dve.wait_ge(s_gm, norm)
                then(dve.tensor_copy(gm[0:p, 0:m, :],
                                     ps[0:p, B_OM, 0:2 * m].rearrange("p (m s) -> p m s", s=2)))
                for i in range(m):
                    then(dve.scalar_tensor_tensor(out=var[0:p, i:i + 1], in0=gm[0:p, i, 0:1],
                                                  scalar=gm[0:p, i, 0:1], in1=gm[0:p, i, 1:2],
                                                  op0=ALU.mult, op1=ALU.subtract))
                dve.tensor_scalar(var[0:p, 0:m], var[0:p, 0:m], -1.0, EPS, ALU.mult,
                                  ALU.add).then_inc(s_var, 1)
                scale_bias(norm, p, m, gm[0:p, 0:m, 0], gamma, beta)

            dve.wait_ge(s_first, 16)
            w1c = fld["w1c"].rearrange("p (t o) -> p t o", t=CT)
            w1m = fld["w1m"].rearrange("p (t g) -> p t g", t=CT)
            dve.tensor_tensor(w1bd[:], w1c[:, :, None, :].to_broadcast([P, CT, GROUPS0, G0]),
                              w1m[:, :, :, None].to_broadcast([P, CT, GROUPS0, G0]),
                              ALU.mult).then_inc(s_wbd, 1)
            then(dve.tensor_copy(mask_x[:].rearrange("p y (x r) -> p (y x) r", r=4),
                                 fld["mask"][0:HID, :, None].to_broadcast([HID, 64, 4])))
            then(dve.tensor_copy(mask[0:HID].rearrange("p (y r x) -> p y r x", r=4, x=W),
                                 mask_x[:, :, None, :].to_broadcast([HID, 8, 4, W])))
            w2c = fld["w2c"].rearrange("p (t o) -> p t o", t=TAPS)
            then(dve.tensor_tensor(w2bd, w2c[:, :, None, :].to_broadcast([P, TAPS, GROUPS0, G0]),
                                   fld["w2m"][:, None, :, None].to_broadcast([P, TAPS, GROUPS0, G0]),
                                   ALU.mult))
            w2 = w2bd.rearrange("p t g o -> p t (g o)")
            then(dve.tensor_copy(w2s[:, :, 0], w2))
            dve.tensor_tensor(w2s[:, :, 1], w2, w2s[:, :, 0].bitcast(F32),
                              ALU.subtract).then_inc(s_wbd, 1)
            dve.tensor_tensor(w3bd[:], fld["w3c"][0:HID, None, :].to_broadcast([HID, GROUPS0, HID]),
                              fld["w3m"][0:HID, :, None].to_broadcast([HID, GROUPS0, HID]),
                              ALU.mult).then_inc(s_wbd, 1)

            dve.wait_ge(s_const, 6)
            for h in range(2):
                dve.wait_ge(s_c1[0], h + 1)
                then(dve.tensor_tensor(half(m0[0:HID], h), ps[0:HID, B_C1 + h, :],
                                       half(mask[0:HID], h), ALU.mult))
                dve.scalar_tensor_tensor(out=half(m0[0:HID], h), in0=half(m0[0:HID], h), scalar=0.0,
                                         in1=half(mask[0:HID], h), op0=ALU.max,
                                         op1=ALU.mult).then_inc(s_masked, 1)
            dve.wait_ge(s_masked, 2)
            for h in range(2):
                dve.wait_ge(s_hi[0], h + 1)
                dve.tensor_tensor(split[HID:P, half_rows(h), 1:1 + W], as_rows(half(m0[0:HID], h)),
                                  split[0:HID, half_rows(h), 1:1 + W].bitcast(F32),
                                  ALU.subtract).then_inc(s_lo[0], 1)
            dve.wait_ge(s_second, 16)
            base = fld["base"].rearrange("p (a t k) -> p a t k", a=3, k=TAPS)
            dve.tensor_copy(sel[:].rearrange("p d a q -> p (d a) q"),
                            fld["sel"][:, :, None].to_broadcast([P, 3 * DENSE, P])).then_inc(s_sel, 1)
            dve.tensor_copy(ramp[:], fld["ramp"][0:1, :]).then_inc(s_sel, 1)
            dbase = fld["dbase"].rearrange("p (a d t) -> p a d t", a=3, d=DENSE)

            def offset_operands(b):
                bo = fld[f"b{b + 1}boff"].rearrange("p (a k) -> p a k", k=TAPS)
                dve.tensor_tensor(dbias[b][:, 0:3 - b], dbase[:, 0:3 - b],
                                  bo[:, 0:3 - b, GTAPS:, None].to_broadcast([P, 3 - b, DENSE, TILES]),
                                  ALU.add).then_inc(s_dbias, 1)
                n = (3 - b) * TAPS
                for a in range(3 - b):
                    dve.tensor_tensor(bias_pos[b][:, a], base[:, a],
                                      bo[:, a, None, :].to_broadcast([P, TILES, TAPS]),
                                      ALU.add).then_inc(s_bpos, 1)
                w = fld[f"b{b + 1}off"].rearrange("p (t o) -> p t o", o=n)
                then(dve.tensor_copy(offw[b][:, :, 0, 0:n], w))
                dve.tensor_tensor(offw[b][:, :, 1, 0:n], w, offw[b][:, :, 0, 0:n].bitcast(F32),
                                  ALU.subtract).then_inc(s_offw, 1)

            offset_operands(0)
            for h in range(2):
                dve.wait_ge(s_low, h + 1)
                then(dve.tensor_tensor(half(m0[0:HID], h), ps[0:HID, B_OM + h, :],
                                       half(m0[0:HID], h), ALU.add))
                dve.scalar_tensor_tensor(out=half(hid[0], h), in0=half(m0[0:HID], h), scalar=0.0,
                                         in1=half(mask[0:HID], h), op0=ALU.max,
                                         op1=ALU.mult).then_inc(s_hid[0], 1)
            for q, (h, m) in enumerate(QUARTERS):
                if m:
                    dve.wait_ge(s_c3[0], q + 1)
                    dve.tensor_scalar(half(x1[:, m, :], h), quarter(m, h), 0.0, None,
                                      ALU.max).then_inc(s_xd[0], 1)
            offset_operands(1)

            def split_image(b):
                for h in range(2):
                    rows = slice(1 + h * H // 2, 1 + (h + 1) * H // 2)
                    src = as_rows(half(feat, h))
                    dve.wait_ge(s_pad[b], h + 1)
                    hi = split[0:HID, rows, 1:1 + W]
                    dve.tensor_copy(hi, src).then_inc(s_hi[b], 1)
                    dve.wait_ge(s_hi[b], h + 1)
                    dve.tensor_tensor(split[HID:P, rows, 1:1 + W], src, hi.bitcast(F32),
                                      ALU.subtract).then_inc(s_lo[b], 1)

            def sampling(b):
                axes = 3 - b
                dve.wait_ge(s_tr, b + 1)
                dve.tensor_copy(feat_t[:, RUN, :], ps[:, B_C1 + 1, 0:HID]).then_inc(s_ftD, 1)
                if b:
                    dve.wait_ge(s_w4, 1)
                if not b:
                    dve.wait_ge(s_bpos, 5)
                for h in range(2):
                    om = (ps[:, B_OM + h, 0:TILES * SLOT]
                          .rearrange("p (t s o) -> p t s o", s=2, o=SLOT))
                    tiles = slice(h * TILES // 2, (h + 1) * TILES // 2)
                    n = slice(h * TILES // 2 * TAPS, (h + 1) * TILES // 2 * TAPS)
                    dve.wait_ge(s_om, 2 * b + h + 1)
                    out_pos = pos[:, 0:axes, n].rearrange("p a (t k) -> p t a k", k=TAPS)
                    for part, other in enumerate((bias_pos[b][:, 0:axes, tiles]
                                                  .rearrange("p a t k -> p t a k"), out_pos)):
                        dve.tensor_tensor(
                            out_pos,
                            om[:, :, part, 0:axes * TAPS].rearrange("p t (a k) -> p t a k", k=TAPS),
                            other, ALU.add).then_inc(s_pos, 1)
                        dve.wait_ge(s_pos, 4 * b + 2 * h + part + 1)
                    then(dve.tensor_scalar(low[:, :, n], pos[:, 0:2, n], -0.5, 0.0, ALU.add, ALU.max))
                    then(dve.tensor_scalar(low[:, :, n], low[:, :, n], MAGIC, MAGIC + W - 2,
                                           ALU.add, ALU.min))
                    then(dve.tensor_scalar(row_y[:, n], low[:, 1, n], MAGIC - TPAD // W, float(W),
                                           ALU.subtract, ALU.mult))
                    dve.scalar_tensor_tensor(out=idx[b][:, n], in0=low[:, 0, n], scalar=MAGIC,
                                             in1=row_y[:, n], op0=ALU.subtract,
                                             op1=ALU.add).then_inc(s_idx, 1)
                for h in range(2):
                    dve.wait_ge(s_omhi, 2 * b + h + 1)
                    dve.tensor_tensor(half(om_split[2 * SLOT:], h), half(om_sb, h),
                                      half(om_split[0:2 * SLOT], h).bitcast(F32),
                                      ALU.subtract).then_inc(s_omlo, 1)
                dve.scalar_tensor_tensor(out=dist[:], in0=low[:], scalar=MAGIC, in1=pos[:, 0:2],
                                         op0=ALU.subtract, op1=ALU.subtract).then_inc(s_dist, 1)
                dve.wait_ge(s_hat, b + 1)
                hy = hat[:, :, 1, :]
                if b == 0:
                    dve.wait_ge(s_sig, 1)
                    then(dve.tensor_tensor(hat_m[:], hat[:, :, 1, :],
                                           sig[:, None, :].to_broadcast([P, 2, TILES * TAPS]), ALU.mult))
                    hy = hat_m[:]
                w4 = corner_w[:].rearrange("p (n y x) -> p n y x", x=2, y=2)
                hx = hat[:, :, 0, :]
                dve.tensor_tensor(
                    w4, hx.rearrange("p r n -> p n r")[:, :, None, :].to_broadcast([P, TILES * TAPS, 2, 2]),
                    hy.rearrange("p r n -> p n r")[:, :, :, None].to_broadcast([P, TILES * TAPS, 2, 2]),
                    ALU.mult).then_inc(s_w4, 1)
                dve.wait_ge(s_w4, b + 1)

            def modulate(i):
                dve.wait_ge(s_hx, i + 1)
                for h in range(2):
                    n, count = turn(0, i, 2, h)
                    dve.wait_ge(s_free[n], count + 1)
                dve.tensor_tensor(hat_x[:, i], hat_x[:, i], mod_x[:], ALU.mult).then_inc(s_hxm, 1)
                dve.wait_ge(s_hxm, i + 1)

            def hidden_stats(h):
                dve.wait_ge(s_c2[1], h + 1)
                then(dve.bn_stats(st[0:HID, 0, h, :], ps[0:HID, B_C1 + h, :]))

            def weigh(b):
                for h in range(2):
                    dve.wait_ge(s_V, 2 * b + h + 1)
                    dve.tensor_copy(half(V[:].rearrange("p t d e -> p (t d e)"), h),
                                    ps[:, B_V + h, :])
                def product(c):
                    cd = b * CHUNKS + c
                    if c % TILES == 0:
                        if b == 0:
                            modulate(c // TILES)
                        else:
                            dve.wait_ge(s_hx, DENSE + c // TILES + 1)
                    dve.wait_ge(s_hy, cd + 1)
                    if cd >= SRING:
                        dve.wait_ge(s_dense, cd - SRING + 1)
                    dve.tensor_tensor(S[cd % SRING], hat_y[cd % HRING], hat_x[:, c // TILES],
                                      ALU.mult).then_inc(s_S, 1)

                for u in range(UNITS):
                    if u == UNITS - 1 and not b:
                        hidden_stats(0)
                    chunks = list(chunks_at(u + 1))
                    t, part = divmod(u, len(PARTS))
                    k0, k1 = PARTS[part]
                    done = b * UNITS + u
                    w = corner_w[:, (t * TAPS + k0) * CORNERS:(t * TAPS + k1) * CORNERS]
                    dve.wait_ge(s_gather[b][t][part], 16 * (k1 - k0))
                    if done >= 2:
                        dve.wait_ge(s_gs, done - 1)
                    dve.tensor_tensor(
                        GW[:, :, k0:k1].rearrange("p c k e -> p k c e"),
                        G[:, (b * TILES + t) % RING, k0:k1].rearrange("p k (c e) -> p k c e", e=HID),
                        w.rearrange("p (k c) -> p k c", c=CORNERS)[:, :, :, None]
                        .to_broadcast([P, k1 - k0, CORNERS, HID]), ALU.mult).then_inc(s_gw, 1)
                    if chunks:
                        product(chunks.pop(0))
                    dve.wait_ge(s_gw, done + 1)
                    dve.tensor_tensor(GA[:, :, k0:k1], GW[:, 0:2, k0:k1], GW[:, 2:4, k0:k1],
                                      ALU.add).then_inc(s_ga, 1)
                    for c in chunks:
                        product(c)
                    dve.wait_ge(s_ga, done + 1)
                    if done >= 4:
                        dve.wait_ge(s_st, done - 3)
                    dve.tensor_tensor(GS[:, t % 2, k0:k1], GA[:, 0, k0:k1], GA[:, 1, k0:k1],
                                      ALU.add).then_inc(s_gs, 1)

            for h in range(2):
                dve.wait_ge(s_c1[1], h + 1)
                then(dve.bn_stats(st[0:HID, 0, h, :], ps[0:HID, B_C1 + h, :]))
            channel_stats(1, HID, 1)
            group_norm(1, HID, 1, fld["gn1s"][0:HID], fld["gn1b"][0:HID])
            split_image(1)
            sampling(0)
            weigh(0)
            hidden_stats(1)
            channel_stats(2, HID, 1)
            group_norm(2, HID, 1, fld["gn2s"][0:HID], fld["gn2b"][0:HID])
            for q, (h, m) in enumerate(QUARTERS):
                dve.wait_ge(s_c3[1], q + 1)
                then(dve.bn_stats(st[:, m, h, :], quarter(m, h)))
            channel_stats(3, P, CT)
            group_norm(3, P, CT, fld["gn3s"], fld["gn3b"])
            for h, m in QUARTERS:
                dve.scalar_tensor_tensor(out=half(x2[:, m, :], h), in0=quarter(m, h),
                                         scalar=sc[:, m:m + 1], in1=half(x1[:, m, :], h),
                                         op0=ALU.mult, op1=ALU.add).then_inc(s_t[1], 1)

            split_image(2)
            sampling(1)
            weigh(1)
            for q, (h, m) in enumerate(LAST_QUARTERS):
                if m:
                    dve.wait_ge(s_c3[2], q + 1)
                    dve.tensor_scalar(half(x3[:, m, :], h), quarter(m, h), fld["b2b3"][:, m:m + 1], 0.0,
                                      ALU.add, ALU.max).then_inc(s_xd[2], 1)

            for h in range(2):
                dve.wait_ge(s_pgm, h + 1)
                tiles = slice(h * TILES // 2, (h + 1) * TILES // 2)
                dve.tensor_tensor(pg[:, tiles], ps[:, B_OM + h, 0:TILES * D]
                                  .rearrange("p (t e) -> p t e", e=2 * D),
                                  fld["pgb"][:, None, :].to_broadcast([P, TILES // 2, 2 * D]),
                                  ALU.add).then_inc(s_pg, 1)
            dve.wait_ge(s_mtm, 1)
            dve.tensor_scalar(mt[:], ps[0:D, B_SMALL, 0:D], 1.0 / N, None, ALU.mult).then_inc(s_mt, 1)
            dve.wait_ge(s_atm, 1)
            dve.tensor_copy(at_w[0:D, :], ps[0:D, B_SMALL, 0:C]).then_inc(s_at, 1)
            for q, (h, m) in enumerate(QUARTERS):
                dve.wait_ge(s_wy, q + 1)
                then(dve.bn_stats(st[:, m, h, :], quarter(m, h)))
            for m in range(CT):
                then(dve.bn_aggr(mv[:, m, :], st[:, m, :, :].rearrange("p a b -> p (a b)")))
            dve.tensor_scalar(var[:], mv[:, :, 1], EPS, None, ALU.add).then_inc(s_var, 1)
            scale_bias(4, P, CT, mv[:, :, 0], fld["bns"], fld["bnb"])
            for h in range(2):
                dve.scalar_tensor_tensor(out=half(yo[:, 1, :], h), in0=quarter(1, h),
                                         scalar=sc[:, 1:2], in1=half(x3[:, 1, :], h),
                                         op0=ALU.mult, op1=ALU.add).then_inc(s_finD, 1)
                dve.wait_ge(s_finA, h + 1)
                dve.tensor_tensor(half(yo[:, 0, :], h), half(yo[:, 0, :], h), half(x3[:, 0, :], h),
                                  ALU.add).then_inc(s_yo[0], 1)

        @block.scalar
        def _(act):
            act.dma_start(x0[:, 0, :], x_in[0]).then_inc(s_x[0], 16)
            act.wait_ge(s_zero, 1)
            act.activation(warm[:], zeros[0:TPAD, 0:1], ACT.Sigmoid)
            act.wait_ge(s_const, 1)
            for h in range(2):
                act.wait_ge(s_masked, h + 1)
                act.activation(split[0:HID, half_rows(h), 1:1 + W], as_rows(half(m0[0:HID], h)),
                               ACT.Copy).then_inc(s_hi[0], 1)
            for h in range(2):
                act.wait_ge(s_c2[0], h + 1)
                act.activation(half(m0[0:HID], h), ps[HID:P, B_OM + h, :], ACT.Copy).then_inc(s_low, 1)
            for q, (h, m) in enumerate(QUARTERS):
                if not m:
                    act.wait_ge(s_c3[0], q + 1)
                    act.activation(half(x1[:, m, :], h), quarter(m, h), ACT.Relu).then_inc(s_xa[0], 1)

            def features(b, scale, bias):
                for h in range(2):
                    act.wait_ge(s_c1[b], h + 1)
                    act.activation(half(feat, h), ps[0:HID, B_C1 + h, :], ACT.Relu,
                                   scale=scale, bias=bias).then_inc(s_pad[b], 1)

            def sampling(b):
                act.wait_ge(s_tr, b + 1)
                act.activation(feat_t[:, 0:RUN, :], ps[:, B_C1, :].rearrange("p (j e) -> p j e", e=HID),
                               ACT.Copy).then_inc(s_ftA, 1)
                act.wait_ge(s_ftA, b + 1)
                act.wait_ge(s_ftD, b + 1)
                act.dma_start(table_view(table[b], 0, 1), table_source()).then_inc(s_tab[b], 16)
                for h in range(2):
                    act.wait_ge(s_omc, 2 * b + h + 1)
                    act.activation(half(om_sb, h), ps[0:2 * SLOT, B_OFF + h, :],
                                   ACT.Copy).then_inc(s_omA, 1)
                for h in range(2):
                    act.wait_ge(s_omA, 2 * b + h + 1)
                    act.activation(half(om_split[0:2 * SLOT], h), half(om_sb, h),
                                   ACT.Copy).then_inc(s_omhi, 1)
                if b == 0:
                    act.wait_ge(s_pos, 4)
                    act.activation(sig[:], pos[:, 2], ACT.Sigmoid).then_inc(s_sig, 1)
                act.wait_ge(s_dist, b + 1)
                for r in range(2):
                    act.activation(absd[:, r], dist[:], ACT.Abs, bias=float(r)).then_inc(s_abs, 1)
                act.wait_ge(s_abs, 2 * b + 2)
                act.activation(hat[:], absd[:], ACT.Relu, scale=-1.0, bias=1.0).then_inc(s_hat, 1)

            def prepare_x(b, i):
                done = b * DENSE + i
                if b:
                    act.wait_ge(s_S, (i + 1) * TILES)
                if done:
                    act.wait_ge(s_hx, done)
                for h in range(2):
                    n, count = turn(b, i, 0, h)
                    act.wait_ge(s_full[n], count + 1)
                    act.activation(half(near_x, h), ps[:, B_D[n], :], ACT.Abs,
                                   bias=dbias[b][:, 0, i, 0:1]).then_inc(s_free[n], 1)
                for h in range(2):
                    n, count = turn(b, i, 0, h)
                    act.wait_ge(s_free[n], count + 1)
                act.activation(hat_x[:, i], near_x[:], ACT.Relu, scale=-1.0, bias=1.0).then_inc(s_hx, 1)

            def prepare_modulation(b, i):
                if i:
                    act.wait_ge(s_hxm, i)
                for h in range(2):
                    n, count = turn(b, i, 2, h)
                    act.wait_ge(s_full[n], count + 1)
                    act.activation(half(mod_x, h), ps[:, B_D[n], :], ACT.Sigmoid,
                                   bias=dbias[b][:, 2, i, 0:1]).then_inc(s_free[n], 1)

            def prepare(b, u):
                for i, axis in prepared_at(u, b):
                    if axis == 0:
                        prepare_x(b, i)
                    if axis == 2:
                        prepare_modulation(b, i)

            def chunk(b, c):
                cd = b * CHUNKS + c
                if c % TILES == 0:
                    act.wait_ge(s_y, 2 * (b * DENSE + c // TILES + 1))
                if cd >= 2:
                    act.wait_ge(s_hy, cd - 1)
                if cd >= HRING:
                    act.wait_ge(s_S, cd - HRING + 1)
                act.activation(near_y[:, c % 2], ps[:, B_Y:B_Y + 2, :].rearrange("p h n -> p (h n)"), ACT.Abs,
                               bias=dbias[b][:, 1, c // TILES, c % TILES:c % TILES + 1]).then_inc(s_ny, 1)
                act.wait_ge(s_ny, cd + 1)
                act.activation(hat_y[cd % HRING], near_y[:, c % 2], ACT.Relu,
                               scale=-1.0, bias=1.0).then_inc(s_hy, 1)

            def hidden(h):
                act.wait_ge(s_c2[2], h + 1)
                act.activation(half(hid[2], h), ps[0:HID, B_C1 + h, :], ACT.Relu,
                               bias=fld["b2b2"][0:HID]).then_inc(s_hid[2], 1)

            def result(h):
                act.wait_ge(s_c3[2], LAST_QUARTERS.index((h, 0)) + 1)
                act.activation(half(x3[:, 0, :], h), quarter(0, h), ACT.Relu,
                               bias=fld["b2b3"][:, 0:1]).then_inc(s_xa[2], 1)

            def phi_g(h):
                act.wait_ge(s_tpg, h + 1)
                act.activation(half(pgT, h), ps[2 * D:4 * D, B_C1 + h, :], ACT.Copy).then_inc(s_pgT, 1)

            def samples(b):
                act.wait_ge(s_dbias, 2)
                prepare(b, -1)
                for u in range(UNITS):
                    for c in chunks_at(u + AHEAD):
                        chunk(b, c)
                    if u == UNITS - 1 and b:
                        hidden(0)
                    t, part = divmod(u, len(PARTS))
                    act.wait_ge(s_st, b * UNITS + u + 1)
                    act.activation(sT[:, t % 2, 2 * part:2 * part + 2], ps[:, B_ST[part], 0:2 * P]
                                   .rearrange("p (q n) -> p q n", n=P), ACT.Copy).then_inc(s_sT, 1)
                    prepare(b, u)

            act.wait_ge(s_sb, 1)
            features(1, sc[0:HID, 0:1], nb[0:HID, 0:1])
            sampling(0)
            samples(0)
            act.wait_ge(s_sb, 2)
            for h in range(2):
                act.activation(half(hid[1], h), ps[0:HID, B_C1 + h, :], ACT.Relu,
                               scale=sc[0:HID, 0:1], bias=nb[0:HID, 0:1]).then_inc(s_hid[1], 1)
            for q, (h, m) in enumerate(QUARTERS):
                act.wait_ge(s_t[1], q + 1)
                act.activation(half(x2[:, m, :], h), half(x2[:, m, :], h), ACT.Relu,
                               bias=nb[:, m:m + 1]).then_inc(s_xd[1] if m else s_xa[1], 1)

            features(2, 1.0, fld["b2b1"][0:HID])
            sampling(1)
            samples(1)
            result(0)
            hidden(1)
            phi_g(0)
            result(1)
            phi_g(1)

            for h in range(2):
                act.activation(half(th[0:D], h), ps[0:D, B_C1 + h, :], ACT.Identity,
                               bias=fld["thb"][0:D]).then_inc(s_th, 1)
            act.wait_ge(s_sb, 1 + 1 + CT + CT)
            for h in range(2):
                act.activation(half(yo[:, 0, :], h), quarter(0, h), ACT.Identity,
                               scale=sc[:, 0:1], bias=nb[:, 0:1]).then_inc(s_finA, 1)
                act.wait_ge(s_finD, h + 1)
                act.activation(half(yo[:, 1, :], h), half(yo[:, 1, :], h), ACT.Identity,
                               bias=nb[:, 1:2]).then_inc(s_yo[1], 1)

        @block.tensor
        def _(pe):
            def keep_clock(bank, n, operand=ident):
                for _ in range(n):
                    pe.matmul(ps[:, bank, 0:P], operand, operand, start=True, stop=True)

            def conv1(b, weights, src, ready):
                m = weights.shape[2]
                for h in range(2):
                    for t in range(CT):
                        pe.wait_ge(ready[t], h + 1)
                        mm = pe.matmul(ps[0:m, B_C1 + h, :], weights[:, t, :], half(src[:, t, :], h),
                                       start=(t == 0), stop=(t == CT - 1))
                    mm.then_inc(s_c1[b], 1)

            def residual(src, quarters):
                for h, m in quarters:
                    pe.matmul(quarter(m, h), ident, half(src[:, m, :], h), start=True, stop=False)

            def conv3(b, weights, start):
                for h in range(2):
                    pe.wait_ge(s_hid[b], h + 1)
                    for m in range(CT):
                        pe.matmul(quarter(m, h), weights[:, m * P:(m + 1) * P], half(hid[b], h),
                                  start=start, stop=True).then_inc(s_c3[b], 1)

            def group_stats(norm, p, m, matrix):
                pe.wait_ge(s_mv, norm)
                pe.matmul(ps[0:p, B_OM, 0:2 * m], matrix[0:p, 0:p],
                          mv[0:p, 0:m, :].rearrange("p m s -> p (m s)"),
                          start=True, stop=True).then_inc(s_gm, 1)

            def features(b):
                pe.wait_ge(s_pad[b + 1], 2)
                for j in range(RUN + 1):
                    tr = pe.transpose(ps[:, B_C1 + j // RUN, (j % RUN) * HID:(j % RUN + 1) * HID],
                                      feat[:, j:j + (P - 1) * RUN + 1:RUN], ident[0:HID, 0:HID])
                tr.then_inc(s_tr, 1)
                keep_clock(7, IDLE[10 + b])
                pe.wait_ge(s_offw, b + 1)

                def to_pixels(h):
                    pe.wait_ge(s_omA, 2 * b + h + 1)
                    for t in range(TILES // 2):
                        om = pe.transpose(ps[:, B_OM + h, t * 2 * SLOT:(t + 1) * 2 * SLOT],
                                          half(om_sb, h)[:, t * P:(t + 1) * P],
                                          ident[0:2 * SLOT, 0:2 * SLOT])
                    om.then_inc(s_om, 1)

                for h in range(2):
                    for k in range(TAPS):
                        if h == 0 and k % 6 == 0:
                            pe.wait_ge(s_lo[b + 1], k // 6 + 1)
                        r = h * H // 2 + k // 3
                        om = pe.matmul(ps[:, B_OFF + h, :],
                                       offw[b][:, k].rearrange("p s o -> p (s o)"),
                                       split[:, r:r + H // 2, k % 3:k % 3 + W],
                                       start=(k == 0), stop=(k == TAPS - 1))
                        if h and k == 3:
                            to_pixels(0)
                    om.then_inc(s_omc, 1)
                to_pixels(1)

            def last_conv3(h, m):
                pe.wait_ge(s_hid[2], h + 1)
                pe.matmul(quarter(m, h), fld["b2w3"][0:HID, m * P:(m + 1) * P], half(hid[2], h),
                          start=False, stop=True).then_inc(s_c3[2], 1)

            def deform(b, weights, dense_weights):
                w = weights.rearrange("p (q o) -> p q o", o=HID)

                for h in range(2):
                    for t in range(4):
                        mm = pe.matmul(ps[:, B_V + h, t * P:(t + 1) * P],
                                       feat[:, (4 * h + t) * P:(4 * h + t + 1) * P],
                                       dense_weights[0:HID, :], start=True, stop=True)
                    mm.then_inc(s_V, 1)

                def positions(u):
                    for i, axis in prepared_at(u, b):
                        for h in range(2):
                            if axis == 1:
                                dst, full = ps[:, B_Y + h, :], s_y
                                if b + i:
                                    pe.wait_ge(s_ny, b * CHUNKS + i * TILES)
                            else:
                                n, count = turn(b, i, axis, h)
                                dst, full = ps[:, B_D[n], :], s_full[n]
                                if count:
                                    pe.wait_ge(s_free[n], count)
                            mm = pe.matmul(dst, sel[:, i, axis, :], half(om_split, h),
                                           start=True, stop=(axis == 2))
                            if axis < 2:
                                own = (ramp[:, None, 0:W] if axis == 0
                                       else ramp[:, h * H // 2:(h + 1) * H // 2, None])
                                mm = pe.matmul(dst, ramp[:, W:],
                                               own.to_broadcast([1, H // 2, W]),
                                               start=False, stop=True)
                            mm.then_inc(full, 1)

                def dense(c):
                    pe.wait_ge(s_S, b * CHUNKS + c + 1)
                    for h in range(2):
                        mm = pe.matmul(ps[0:HID, B_C1 + h, :], V[:, c % TILES, c // TILES, :],
                                       half(S[(b * CHUNKS + c) % SRING], h), start=(c == 0),
                                       stop=(c == CHUNKS - 1 and h == 0))
                        if c == CHUNKS - 1 and h == 0:
                            mm.then_inc(s_c2[b + 1], 1)
                    mm.then_inc(s_dense, 1)

                def pairs(u):
                    return range(u % 2 * 2, u % 2 * 2 + 2)

                def contract(u):
                    t = u // len(PARTS)
                    pe.wait_ge(s_sT, b * UNITS + u + 1)
                    for q in pairs(u):
                        mm = pe.matmul(ps[0:HID, B_C1 + t // 4, t % 4 * P:(t % 4 + 1) * P], w[:, q, :],
                                       sT[:, t % 2, q], start=False, stop=(u == UNITS - 1 and q == PAIRS))
                    if u == UNITS - 1:
                        mm.then_inc(s_c2[b + 1], 1)

                if b == 0:
                    pe.wait_ge(s_sel, 2)
                pe.wait_ge(s_omlo, 2 * b + 2)
                positions(-1)

                def residual_at(u):
                    i = u - (UNITS - len(RESIDUAL))
                    return QUARTERS[sum(RESIDUAL[:i]):sum(RESIDUAL[:i + 1])] if i >= 0 else []

                for u in range(UNITS):
                    for c in chunks_at(u):
                        dense(c)
                    if b:
                        residual(x2, residual_at(u))
                    t, part = divmod(u, len(PARTS))
                    done = b * UNITS + u
                    if u >= LAG:
                        contract(u - LAG)
                    if u == UNITS - 1:
                        for late in range(u - LAG + 1, u):
                            contract(late)
                    pe.wait_ge(s_gs, done + 1)
                    if done >= 2:
                        pe.wait_ge(s_sT, done - 1)
                    for q in pairs(u):
                        k = min(2 * q, GTAPS - 2)
                        mm = pe.transpose(ps[:, B_ST[part], q % 2 * P:(q % 2 + 1) * P],
                                          GS[:, t % 2, k:k + 2, :].rearrange("p k e -> p (k e)"), ident)
                    mm.then_inc(s_st, 1)
                    if u < BESIDE.index(1):
                        keep_clock(0, IDLE[8 + u])
                    positions(u)
                if b:
                    last_conv3(0, 1)
                    last_conv3(0, 0)
                contract(UNITS - 1)

            tpgw = fld["tpgw"].rearrange("p (t e) -> p t e", e=4 * D)

            def theta_phi_g(h):
                first = [m for half_of, m in LAST_QUARTERS if half_of == h]
                for i in first:
                    pe.wait_ge(s_xd[2] if i else s_xa[2], h + 1)
                    mm = pe.matmul(ps[0:4 * D, B_C1 + h, :], tpgw[:, i, :], half(x3[:, i, :], h),
                                   start=(i == first[0]), stop=(i == first[-1]))
                mm.then_inc(s_tpg, 1)

            def phi_g_to_pixels(h):
                pe.wait_ge(s_pgT, h + 1)
                for t in range(TILES // 2):
                    tr = pe.transpose(ps[:, B_OM + h, t * 2 * D:(t + 1) * 2 * D],
                                      half(pgT, h)[:, t * P:(t + 1) * P], ident[0:2 * D, 0:2 * D])
                tr.then_inc(s_pgm, 1)

            pe.wait_ge(s_zero, 1)
            keep_clock(7, IDLE[0], zeros[:])
            pe.wait_ge(s_first, 16)
            pe.wait_ge(s_wbd, 1)
            for t in range(CT):
                pe.wait_ge(s_x[t], 16)
                for h in range(2):
                    mm = pe.matmul(ps[0:HID, B_C1 + h, :], w1bd[:, t].rearrange("p g o -> p (g o)"),
                                   half(x0[:, t, :], h), start=(t == 0), stop=(t == CT - 1))
                    if t == CT - 1:
                        mm.then_inc(s_c1[0], 1)
            residual(x0, QUARTERS[:3])
            pe.wait_ge(s_wbd, 2)
            for h in range(2):
                for k in range(TAPS):
                    if h == 0 and k % 6 == 0:
                        pe.wait_ge(s_lo[0], k // 6 + 1)
                    r0 = h * H // 2 + k // 3
                    mm = pe.matmul(ps[:, B_OM + h, :], w2s[:, k].rearrange("p s o -> p (s o)"),
                                   split[:, r0:r0 + H // 2, k % 3:k % 3 + W],
                                   start=(k == 0), stop=(k == TAPS - 1))
                mm.then_inc(s_c2[0], 1)
            residual(x0, QUARTERS[3:])
            pe.wait_ge(s_wbd, 3)
            conv3(0, w3bd[:].rearrange("p g o -> p (g o)"), False)

            pe.wait_ge(s_second, 16)
            conv1(1, fld["b1w1"].rearrange("p (t o) -> p t o", o=HID), x1, (s_xa[0], s_xd[0]))
            keep_clock(7, IDLE[1])
            group_stats(1, HID, 1, fld["g2"])
            keep_clock(7, IDLE[2])
            features(0)
            deform(0, fld["b1w2"], fld["b1wd"])
            keep_clock(7, IDLE[3])
            group_stats(2, HID, 1, fld["g2"])
            keep_clock(7, IDLE[4])
            conv3(1, fld["b1w3"][0:HID], True)
            keep_clock(0, IDLE[5])
            group_stats(3, P, CT, fld["g8"])
            keep_clock(0, IDLE[6])

            conv1(2, fld["b2w1"].rearrange("p (t o) -> p t o", o=HID), x2, (s_xa[1], s_xd[1]))
            keep_clock(7, IDLE[7])
            features(1)
            deform(1, fld["b2w2"], fld["b2wd"])
            theta_phi_g(0)
            last_conv3(1, 0)
            last_conv3(1, 1)

            phi_g_to_pixels(0)
            theta_phi_g(1)
            keep_clock(7, IDLE[13])
            phi_g_to_pixels(1)
            keep_clock(7, IDLE[14])
            pe.wait_ge(s_pg, 2)
            for t in range(TILES):
                mm = pe.matmul(ps[0:D, B_SMALL, 0:D], pg[:, t, D:2 * D], pg[:, t, 0:D],
                               start=(t == 0), stop=(t == TILES - 1))
            mm.then_inc(s_mtm, 1)
            keep_clock(7, IDLE[15])
            pe.wait_ge(s_mt, 1)
            pe.matmul(ps[0:D, B_SMALL, 0:C], mt[:], fld["www"][0:D], start=True, stop=True).then_inc(s_atm, 1)
            keep_clock(2, IDLE[12])
            pe.wait_ge(s_at, 1)
            pe.wait_ge(s_wb, 16)
            pe.wait_ge(s_th, 2)
            for h, m in QUARTERS:
                pe.matmul(quarter(m, h), at_w[:, m * P:(m + 1) * P], half(th[0:D + 1], h),
                          start=True, stop=True).then_inc(s_wy, 1)


def constants():
    import numpy as np

    p = np.arange(P)
    w1m = np.zeros((P, CT, GROUPS0), np.float32)
    for t in range(CT):
        w1m[p, t, 2 * t + p // HID] = 1
    wm = np.zeros((P, GROUPS0), np.float32)
    wm[p, p % HID // G0] = 1
    k = np.arange(TAPS)
    base = np.zeros((P, 3, TILES, TAPS), np.float32)
    t = np.arange(TILES)[None, :, None]
    base[:, 0] = (p % W)[:, None, None] + k % 3 - 1 + 0 * t
    base[:, 1] = (p // W)[:, None, None] + ROWS * t + k // 3 - 1
    dbase = np.zeros((P, 3, DENSE, TILES), np.float32)
    dbase[:, 0] = (GTAPS + np.arange(DENSE))[None, :, None] % 3 - 1 - (p % W)[:, None, None]
    dbase[:, 1] = ((GTAPS + np.arange(DENSE))[None, :, None] // 3 - 1 - (p // W)[:, None, None]
                   - ROWS * np.arange(TILES)[None, None, :])
    sel = np.zeros((P, DENSE, 3), np.float32)
    for i in range(DENSE):
        for axis in range(3):
            sel[np.arange(4) * SLOT + axis * TAPS + GTAPS + i, i, axis] = 1
    ramp = np.concatenate([np.arange(W), np.ones(P)])[None].astype(np.float32)
    return {"w1m": w1m, "w2m": wm, "w3m": wm, "ident": np.eye(P, dtype=np.float32),
            "g2": np.kron(np.eye(P // 2), np.full((2, 2), 1 / 2)).astype(np.float32),
            "g8": np.kron(np.eye(P // 8), np.full((8, 8), 1 / 8)).astype(np.float32),
            "base": base, "dbase": dbase, "sel": sel, "ramp": ramp}


def pack(fields, parts):
    import numpy as np

    packed = np.zeros((P, width(fields)), np.float32)
    at = 0
    for name, n in fields:
        a = parts[name]
        a = a.reshape(a.shape[0], -1)
        packed[:a.shape[0], at:at + a.shape[1]] = a
        at += n
    return packed


def lay_out(i):
    import numpy as np

    def col(v):
        return v.reshape(-1, P).T

    def twice(v):
        return np.concatenate([v, v]).reshape(P, 1)

    def taps(w):
        return np.tile(w.reshape(w.shape[0], HID, TAPS).transpose(1, 2, 0), (2, 1, 1))

    def channels(w):
        return w.reshape(w.shape[0], CT, P).transpose(2, 1, 0)

    def dense(w):
        return w.reshape(HID, HID, TAPS)[:, :, GTAPS:].transpose(1, 2, 0)

    def pairs(w):
        w = w.reshape(HID, HID, TAPS).transpose(2, 1, 0)[:GTAPS]
        w = np.concatenate([w[:-1], np.zeros_like(w[:1]), w[-1:]], 0)
        return w.reshape(PAIRS + 1, P, HID).transpose(1, 0, 2)

    def rows(v):
        return np.broadcast_to(v.reshape(1, -1), (P, v.size))

    xy = [2 * k + 1 for k in range(TAPS)] + [2 * k for k in range(TAPS)]
    w1 = i["L0_conv_w1"].reshape(CT, 2, G0, HID).transpose(1, 3, 0, 2).reshape(P, CT * G0)
    m = i["L0_conv_mask"].reshape(GROUPS0, 64)
    w3 = i["L0_conv_w3"].reshape(GROUPS0, HID, G0).transpose(0, 2, 1).reshape(HID, HID)
    w2 = taps(i["L0_conv_w2"].reshape(GROUPS0, G0, G0, 3, 3).transpose(1, 0, 2, 3, 4)
              .reshape(G0, HID, 3, 3))
    parts = dict(constants())
    parts.update({
        "w1c": w1, "mask": np.tile(np.repeat(m, G0, 0), (2, 1)), "w2c": w2, "w3c": w3,
        "b1w1": channels(i["L1_conv_w1"].reshape(HID, C)), "b1off": taps(i["L1_conv_w_off"]),
        "b1boff": rows(i["L1_conv_b_off"]), "b1w2": pairs(i["L1_conv_w2"]),
        "b1wd": dense(i["L1_conv_w2"]), "b2wd": dense(i["L2_conv_w2"]),
        "b1w3": i["L1_conv_w3"].reshape(C, HID).T,
        "gn1s": twice(i["L1_conv_gn1_scale"]), "gn1b": twice(i["L1_conv_gn1_bias"]),
        "gn2s": twice(i["L1_conv_gn2_scale"]), "gn2b": twice(i["L1_conv_gn2_bias"]),
        "gn3s": col(i["L1_conv_gn3_scale"]), "gn3b": col(i["L1_conv_gn3_bias"]),
        "b2w1": channels(i["L2_conv_w1"].reshape(HID, C)), "b2off": taps(i["L2_conv_w_off"][xy]),
        "b2boff": rows(i["L2_conv_b_off"][xy]), "b2w2": pairs(i["L2_conv_w2"]),
        "b2w3": i["L2_conv_w3"].reshape(C, HID).T,
        "b2b1": twice(i["L2_conv_b1"]), "b2b2": twice(i["L2_conv_b2"]), "b2b3": col(i["L2_conv_b3"]),
        "tpgw": channels(np.concatenate([i["L3_conv_theta_w"], i["L3_conv_theta_w"],
                                         i["L3_conv_phi_w"], i["L3_conv_g_w"]])),
        "pgb": rows(np.concatenate([i["L3_conv_phi_b"], i["L3_conv_g_b"]])),
        "thb": i["L3_conv_theta_b"].reshape(D, 1),
        "www": i["L3_conv_w_w"].T, "bns": col(i["L3_conv_bn_gamma"]), "bnb": col(i["L3_conv_bn_beta"]),
    })
    return {"x": i["x"].reshape(CT, P, N), "first": pack(FIRST, parts), "second": pack(SECOND, parts),
            "w_b": i["L3_conv_w_b"].reshape(1, C)}


def kernel(**inputs):
    import numpy as np
    import concourse.bacc as bacc
    from concourse.bass_utils import run_bass_kernel_spmd as run

    arrays = {f"in_{k}": np.ascontiguousarray(v)
              for k, v in lay_out({k: np.asarray(v) for k, v in inputs.items()}).items()}
    nc = bacc.Bacc("TRN2", target_bir_lowering=False, num_devices=1)
    args = [nc.dram_tensor(k, a.shape, mybir.dt.from_np(a.dtype), kind="ExternalInput").ap()
            for k, a in arrays.items()]
    out = nc.dram_tensor("out", (CT, P, N), F32, kind="ExternalOutput").ap()
    conv_chain(nc, *args, out)
    r = run(nc, [arrays], core_ids=[0])
    return r.results[0]["out"].reshape(1, C, H, W)
```
